# Optimizing a Trainium2 kernel written in Bass

```python
import numpy as np
import jax
import jax.numpy as jnp

def _softmax(x, axis=-1):
    return jax.nn.softmax(x, axis=axis)

def _gelu(x):
    return jax.nn.gelu(x, approximate=True)

def _silu(x):
    return jax.nn.silu(x)

def _sigmoid(x):
    return jax.nn.sigmoid(x)

def _layernorm(x, axis=-1, eps=1e-05):
    m = jnp.mean(x, axis=axis, keepdims=True)
    v = jnp.var(x, axis=axis, keepdims=True)
    return (x - m) / jnp.sqrt(v + eps)

def _scatter_add(tgt, idx, src, axis=0):
    return tgt.at[idx].add(src)

def _segment_sum(src, seg, n):
    return jax.ops.segment_sum(src, seg, n)
kernel_name = 'mk_seq_preln_d1_jaxref_r8_cb554c'

def setup_inputs(seed: int=0):
    np.random.seed(seed)
    _w = jnp.asarray

    def _L0_attn_setup():
        import jax, jax.numpy as jnp
        import numpy as np
        D_MODEL = 256
        N_HEADS = 16
        N_KV = 4
        GROUP = N_HEADS // N_KV
        D_K = D_MODEL // N_HEADS
        D_V = D_MODEL // N_KV
        THETA = 10000.0
        Q_DIM = N_HEADS * D_K
        K_DIM = N_KV * D_K
        V_DIM = N_KV * D_V

        def _apply_rope(t, sin, cos):
            half = t.shape[-1] // 2
            x1, x2 = (t[..., :half], t[..., half:])
            rot = jnp.concatenate([-x2, x1], axis=-1)
            return t * cos + rot * sin
        key = jax.random.key(seed)
        k1, k2, k3 = jax.random.split(key, 3)
        x = jax.random.normal(k1, (2, 256, D_MODEL), dtype=jnp.float32)
        W_attn = jax.random.normal(k2, (D_MODEL, Q_DIM + K_DIM + V_DIM), dtype=jnp.float32) * 0.02
        W_out = jax.random.normal(k3, (N_HEADS * D_V, D_MODEL), dtype=jnp.float32) * 0.02
        b_out = jnp.zeros((D_MODEL,), dtype=jnp.float32)
        return {'x': x, 'W_attn': W_attn, 'W_out': W_out, 'b_out': b_out}
    _L0_attn_in = _L0_attn_setup()

    def _L0_ffn_setup():
        import jax, jax.numpy as jnp
        import numpy as np
        B, S, D, E, R, TOP_K = (4, 512, 256, 6, 16, 2)
        key = jax.random.key(seed)
        ks = jax.random.split(key, 9)
        scale = 0.02
        return {'x': jax.random.normal(ks[0], (B, S, D), dtype=jnp.float32), 'W_base': jax.random.normal(ks[1], (D, D), dtype=jnp.float32) * scale, 'b_base': jax.random.normal(ks[2], (D,), dtype=jnp.float32) * scale, 'A_s': jax.random.normal(ks[3], (D, R), dtype=jnp.float32) * scale, 'B_s': jax.random.normal(ks[4], (R, D), dtype=jnp.float32) * scale, 'A_r': jax.random.normal(ks[5], (E, D, R), dtype=jnp.float32) * scale, 'B_r': jax.random.normal(ks[6], (E, R, D), dtype=jnp.float32) * scale, 'W_router': jax.random.normal(ks[7], (D, E), dtype=jnp.float32) * scale, 'b_router': jax.random.normal(ks[8], (E,), dtype=jnp.float32) * scale}
    _L0_ffn_in = _L0_ffn_setup()
    _d = {'L0_attn_x': _L0_attn_in['x'], 'L0_attn_W_attn': _L0_attn_in['W_attn'], 'L0_attn_W_out': _L0_attn_in['W_out'], 'L0_attn_b_out': _L0_attn_in['b_out'], 'L0_ffn_W_base': _L0_ffn_in['W_base'], 'L0_ffn_b_base': _L0_ffn_in['b_base'], 'L0_ffn_A_s': _L0_ffn_in['A_s'], 'L0_ffn_B_s': _L0_ffn_in['B_s'], 'L0_ffn_A_r': _L0_ffn_in['A_r'], 'L0_ffn_B_r': _L0_ffn_in['B_r'], 'L0_ffn_W_router': _L0_ffn_in['W_router'], 'L0_ffn_b_router': _L0_ffn_in['b_router']}
    _x0 = _d['L0_attn_x']
    _d['L0_attn_x'] = jax.random.normal(jax.random.fold_in(jax.random.key(seed), 1), (4, 1024, 256), dtype=_x0.dtype)
    del _x0
    return _d

def reference(L0_attn_x, L0_attn_W_attn, L0_attn_W_out, L0_attn_b_out, L0_ffn_W_base, L0_ffn_b_base, L0_ffn_A_s, L0_ffn_B_s, L0_ffn_A_r, L0_ffn_B_r, L0_ffn_W_router, L0_ffn_b_router):

    def _L0_attn_ref(x, W_attn, W_out, b_out):
        import jax, jax.numpy as jnp
        import numpy as np
        D_MODEL = 256
        N_HEADS = 16
        N_KV = 4
        GROUP = N_HEADS // N_KV
        D_K = D_MODEL // N_HEADS
        D_V = D_MODEL // N_KV
        THETA = 10000.0
        Q_DIM = N_HEADS * D_K
        K_DIM = N_KV * D_K
        V_DIM = N_KV * D_V

        def _apply_rope(t, sin, cos):
            half = t.shape[-1] // 2
            x1, x2 = (t[..., :half], t[..., half:])
            rot = jnp.concatenate([-x2, x1], axis=-1)
            return t * cos + rot * sin
        B, L, _ = x.shape
        qkv = x @ W_attn
        q = qkv[..., :Q_DIM].reshape(B, L, N_HEADS, D_K).transpose(0, 2, 1, 3)
        k = qkv[..., Q_DIM:Q_DIM + K_DIM].reshape(B, L, N_KV, D_K).transpose(0, 2, 1, 3)
        v = qkv[..., Q_DIM + K_DIM:].reshape(B, L, N_KV, D_V).transpose(0, 2, 1, 3)
        inv_freq = 1.0 / THETA ** (jnp.arange(0, D_K, 2, dtype=jnp.float32) / D_K)
        freqs = jnp.arange(L, dtype=jnp.float32)[:, None] * inv_freq[None, :]
        ang = jnp.concatenate([freqs, freqs], axis=-1)
        sin, cos = (jnp.sin(ang), jnp.cos(ang))
        q = _apply_rope(q.astype(jnp.float32), sin, cos).astype(x.dtype)
        k = _apply_rope(k.astype(jnp.float32), sin, cos).astype(x.dtype)
        qg = q.reshape(B, N_KV, GROUP, L, D_K)
        scores = jnp.einsum('bkgqd,bkld->bkgql', qg, k) / D_K ** 0.5
        probs = jax.nn.softmax(scores, axis=-1)
        ctx = jnp.einsum('bkgql,bkle->bkgqe', probs, v)
        ctx = ctx.reshape(B, N_HEADS, L, D_V).transpose(0, 2, 1, 3).reshape(B, L, N_HEADS * D_V)
        return ctx @ W_out + b_out

    def _L0_ffn_ref(x, W_base, b_base, A_s, B_s, A_r, B_r, W_router, b_router):
        import jax, jax.numpy as jnp
        import numpy as np
        B, S, D, E, R, TOP_K = (4, 512, 256, 6, 16, 2)
        base_out = jax.lax.stop_gradient(jnp.einsum('bsd,df->bsf', x, W_base) + b_base)
        shared_out = jnp.einsum('bsr,rf->bsf', jnp.einsum('bsd,dr->bsr', x, A_s), B_s)
        gates = jax.nn.softmax(jnp.einsum('bsd,de->bse', x, W_router) + b_router, axis=-1)
        topk_w, topk_i = jax.lax.top_k(gates, TOP_K)
        w_per_e = jnp.sum(topk_w[..., None] * jax.nn.one_hot(topk_i, E, dtype=x.dtype), axis=2)
        h = jnp.einsum('bsd,edr->bser', x, A_r)
        hw = h * w_per_e[..., None]
        routed_out = jnp.einsum('bser,erf->bsf', hw, B_r)
        return base_out + shared_out + routed_out
    x = L0_attn_x
    x = x + _L0_attn_ref(_layernorm(x, axis=-1), L0_attn_W_attn, L0_attn_W_out, L0_attn_b_out)
    x = x + _L0_ffn_ref(_layernorm(x, axis=-1), L0_ffn_W_base, L0_ffn_b_base, L0_ffn_A_s, L0_ffn_B_s, L0_ffn_A_r, L0_ffn_B_r, L0_ffn_W_router, L0_ffn_b_router)
    return x

_drawn_inputs = setup_inputs


def setup_inputs(seed=0):
    import zlib

    import numpy as np

    out = dict(_drawn_inputs(seed))
    spreads = {'L0_attn_b_out': (0.0, 0.718)}
    factors = {'L0_attn_W_attn': 8.0,
     'L0_attn_W_out': 8.0,
     'L0_ffn_b_base': 23.416,
     'L0_ffn_A_r': 7.5,
     'L0_ffn_B_r': 7.496,
     'L0_ffn_W_router': 8.0,
     'L0_ffn_b_router': 36.079,
     'L0_ffn_A_s': 8.0,
     'L0_ffn_B_s': 8.0}
    for name, (base, spread) in spreads.items():
        noise = np.random.default_rng([zlib.crc32(name.encode()), seed]).standard_normal(out[name].shape)
        drawn = base * np.exp(spread * noise) if base else spread * noise
        out[name] = jnp.asarray(drawn.astype(out[name].dtype))
    for name, factor in factors.items():
        out[name] = (out[name] * factor).astype(out[name].dtype)
    return out
```

```python
from contextlib import ExitStack, contextmanager

import concourse.bass as bass
from concourse import mybir

F32 = mybir.dt.float32
BF16 = mybir.dt.bfloat16
ALU = mybir.AluOpType
ACT = mybir.ActivationFunctionType
AX = mybir.AxisListType

P = 128
B, L, D = 4, 1024, 256
HEADS, KV = 16, 4
HPG = HEADS // KV
DK, DV = D // HEADS, D // KV
QK = HEADS * DK + KV * DK
QKV = QK + KV * DV
DC = D // P
TILES = B * L // P
TPB = L // P
HALF = TPB // 2
HT = HALF * P
GROUPS = B * KV
EPS = 1e-5
SCALE = DK ** -0.5

Q_PART = (0, 0, 1, 0, 1, 2)
K_PART = (0, 1, 0, 2, 1, 0)
SLOTS = len(Q_PART)
KS = SLOTS * DK
NSH = 3

E, R, TOP_K = 6, 16, 2
NLR = R + E * R
NF = D + NLR + E
STEPS = 2 * 2 * TPB
LEAD = 24
RING = 8
NFETCH = 2 * SLOTS + 2
NMISC = 6
FSET = 2
SETS = TILES // FSET
FREE = 2


@contextmanager
def rounds(nc, eng, end, step):
    with eng.Fori(0, end, step) as i:
        yield nc.s_assert_within(i, 0, end - step,
                                 skip_runtime_bounds_check_because="step divides end")


def layer_kernel(nc, x, w_attn, w_out, b_out, w_base, b_base, a_s, b_s, a_r, b_r,
                 w_router, b_router, rope, ident, before, out):
    x_t = x.rearrange("b (t p) d -> p (b t) d", p=P)
    out_t = out.rearrange("b (t p) d -> p (b t) d", p=P)

    with ExitStack() as ctx:
        def sb(name, shape, dt=F32):
            return ctx.enter_context(nc.sbuf_tensor(name, shape, dt))

        def sem(name):
            return ctx.enter_context(nc.semaphore(name))

        q_dram = nc.dram_tensor("q_parts", [B, SLOTS, HEADS * DK, L], BF16).ap()
        k_dram = nc.dram_tensor("k_parts", [B, SLOTS, KV * DK, L], BF16).ap()
        v_dram = nc.dram_tensor("v_rows", [B, KV, P, TPB * DV], F32).ap()

        xs = sb("xs", [P, TILES, D])
        wa = sb("wa", [P, DC, QKV])
        wf = sb("wf", [P, DC, NF])
        wlr = sb("wlr", [NLR + 1, D])
        bo_row = sb("bo_row", [P, D])
        br_row = sb("br_row", [P, E])
        rope_sb = sb("rope_sb", [P, TPB, 2, DK])
        id32 = sb("id32", [P, P])
        id16 = sb("id16", [P, P], BF16)
        before_sb = sb("before_sb", [P, E * E])

        stats = sb("stats", [P, 4, 6])
        moments = sb("moments", [P, 4, 2])
        var_eps = sb("var_eps", [P, 4])
        rstd = sb("rstd", [P, 4])
        neg_half = sb("neg_half", [P, 2])
        xhat = sb("xhat", [P, 2, D])
        xhat_t = sb("xhat_t", [P, 2, DC, P])

        qk = sb("qk", [P, 2, QK])
        rope_c = sb("rope_c", [P, QK])
        rope_s = sb("rope_s", [P, QK])
        qkr = sb("qkr", [P, 2, QK])
        qk_t = sb("qk_t", [P, 2, DC + 1, P])
        rest = sb("rest", [P, 2, DC + 1, P])
        parts = sb("parts", [P, 2, 3, DC + 1, HT], BF16)
        v_out = sb("v_out", [P, 2, KV, HALF * DV])

        q3 = [sb(f"q3_{e}", [P, HPG, L], BF16) for e in range(2)]
        k3 = [sb(f"k3_{e}", [P, L], BF16) for e in range(2)]
        vg = [sb(f"vg_{e}", [P, TPB, DV]) for e in range(2)]
        wo = [sb(f"wo_{e}", [P, 2, D]) for e in range(2)]
        probs = sb("probs", [P, RING, 2, HT])
        negm = sb("negm", [P, 2, 2 * TPB])
        den = sb("den", [P, 2, 2 * TPB])
        lnden = sb("lnden", [P, 2, 2 * TPB])
        shift = sb("shift", [P, 2 * TPB])
        shift_rest = sb("shift_rest", [P, 2 * TPB])
        shift_parts = sb("shift_parts", [P, TPB, 2, NSH], BF16)
        shift_rows = [sb(f"shift_rows_{q}", [2 * NSH, L], BF16) for q in range(2)]
        ctx_t = sb("ctx_t", [P, 2, L])

        lg = sb("lg", [P, 2, FSET, E])
        lmax = sb("lmax", [P, 2, FSET])
        lexp = sb("lexp", [P, 2, FSET, E])
        lsum = sb("lsum", [P, 2, FSET])
        linv = sb("linv", [P, 2, FSET])
        gates = sb("gates", [P, 2, FSET, E])
        cge = sb("cge", [P, 2, FSET * E, E])
        cgt = sb("cgt", [P, 2, FSET * E, E])
        rank = sb("rank", [P, 2, FSET, E])
        wexp = sb("wexp", [P, 2, FSET, E])
        hw = sb("hw", [P, 2, FSET, NLR + 1])
        hw_t = sb("hw_t", [NLR + 1, 2, FSET, P])
        y = sb("y", [P, 2, FSET, D])

        apart = sem("apart")
        ps = ctx.enter_context(nc.psum_tensor("ps", [P, 8, 512], F32))

        weights_in = sem("weights_in")
        x_in = sem("x_in")
        consts = sem("consts")
        a_norm = sem("a_norm")
        a_var = sem("a_var")
        a_rstd = sem("a_rstd")
        a_xhat = sem("a_xhat")
        a_xt = sem("a_xt")
        a_xts = sem("a_xts")
        a_proj = sem("a_proj")
        a_qk = sem("a_qk")
        a_v = sem("a_v")
        a_rope = sem("a_rope")
        a_roped = sem("a_roped")
        a_qkt = sem("a_qkt")
        a_qkts = sem("a_qkts")
        a_part0 = sem("a_part0")
        a_rest = sem("a_rest")
        a_part1 = sem("a_part1")
        a_split = sem("a_split")
        a_stored = [sem(f"a_stored{e}") for e in range(2)]
        nweights = 6 + 2 * DC + 4
        nstores = 3 * SLOTS + 1
        bank_xt, bank_qk, bank_v, bank_qkt = 0, 2, 4, 6

        def pipelined(eng, step, lead):
            for u in range(-lead, 0):
                step(0, u)
            with rounds(nc, eng, B - 1, 1) as b:
                for u in range(TPB):
                    step(b, u)
            for u in range(TPB):
                step(B - 1, u)

        def exists(t):
            return not isinstance(t, int) or 0 <= t < TILES

        with nc.Block() as block:
            @block.sync
            def _(sp):
                def load_x(hb):
                    sp.dma_start(xs[:, bass.ts(hb, HALF), :],
                                 x_t[:, bass.ts(hb, HALF), :]).then_inc(x_in, 16)

                def store(b, par):
                    hb = 2 * b + par
                    sp.wait_ge(a_split, HALF * (hb + 1))
                    sp.sem_inc(apart, 1)
                    sp.wait_ge(a_v, FREE + HALF * (hb + 1))
                    sp.sem_inc(apart, 1)
                    cols = slice(par * HT, (par + 1) * HT)
                    for s in range(SLOTS):
                        for c in range(DC):
                            sp.dma_start(q_dram[b, s, c * P:(c + 1) * P, cols],
                                         parts[:, par, Q_PART[s], c, :]).then_inc(a_stored[par], 16)
                        sp.dma_start(k_dram[b, s, :, cols],
                                     parts[0:KV * DK, par, K_PART[s], DC, :]).then_inc(a_stored[par], 16)
                    vcols = slice(par * HALF * DV, (par + 1) * HALF * DV)
                    sp.dma_start(v_dram[b, :, :, vcols].rearrange("g p n -> p g n"),
                                 v_out[:, par, :, :]).then_inc(a_stored[par], 16)

                def half_row(b, par, last=False):
                    hb = 2 * b + par
                    sp.wait_ge(x_in, 16 * (hb + 1))
                    sp.sem_inc(apart, 1)
                    if not last:
                        load_x(hb + 1)
                    store(b, par)

                load_x(0)
                with rounds(nc, sp, B - 1, 1) as b:
                    half_row(b, 0)
                    half_row(b, 1)
                half_row(B - 1, 0)
                half_row(B - 1, 1, last=True)
                for par in range(2):
                    sp.wait_ge(a_stored[par], 1 + 16 * nstores * B)

            @block.gpsimd
            def _(pool):
                pool.sem_inc(a_roped, FREE)
                pool.wait_ge(consts, 7)
                pool.wait_ge(weights_in, 16 * nweights)
                nh, half = QK // DK, DK // 2

                def rotate(t, u):
                        p = u % 2
                        xv = qk[:, p, :].rearrange("p (h i) -> p h i", i=DK)
                        cv = rope_c[:, :].rearrange("p (h i) -> p h i", i=DK)
                        sv = rope_s[:, :].rearrange("p (h i) -> p h i", i=DK)

                        def table(k, lo, hi):
                            return rope_sb[:, u:u + 1, k, lo:hi].to_broadcast([P, nh, hi - lo])

                        pool.wait_ge(a_xhat, t + 1)
                        nc.gpsimd.tensor_tensor(xs[:, t, :], xs[:, t, :], bo_row[:, :], ALU.add)
                        pool.wait_ge(a_qk, FREE + t + 1)
                        pool.wait_ge(a_roped, FREE + t)
                        nc.gpsimd.tensor_tensor(cv, xv, table(0, 0, DK), ALU.mult).then_inc(a_rope, 1)
                        nc.gpsimd.tensor_tensor(sv[:, :, 0:half], xv[:, :, half:DK], table(1, 0, half),
                                                ALU.mult).then_inc(a_rope, 1)
                        nc.gpsimd.tensor_tensor(sv[:, :, half:DK], xv[:, :, 0:half], table(1, half, DK),
                                                ALU.mult).then_inc(a_rope, 1)
                        pool.wait_ge(a_rope, 3 * (t + 1))
                        pool.wait_ge(a_qkt, FREE + t - 1)
                        nc.gpsimd.tensor_tensor(qkr[:, p, :], rope_c[:, :], rope_s[:, :],
                                                ALU.add).then_inc(a_roped, 1)

                def step(b, u):
                    t = TPB * b + u
                    if exists(t + 3):
                        slot = slice(1 - u % 2, 2 - u % 2)
                        pool.wait_ge(a_var, t + 4)
                        nc.gpsimd.tensor_tensor(rstd[:, slot], var_eps[:, slot], neg_half[:, 0:1],
                                                ALU.pow).then_inc(a_rstd, 1)
                    if exists(t + 1):
                        rotate(t + 1, (u + 1) % TPB)

                pipelined(pool, step, 3)

            @block.vector
            def _(dve):
                for e in range(2):
                    nc.vector.memset(qk_t[KV * DK:P, e, DC, :], 0.0).then_inc(consts, 1)
                    nc.vector.memset(k3[e][KS:P, :], 1.0).then_inc(consts, 1)
                nc.vector.memset(hw[:, :, :, NLR:NLR + 1], 1.0).then_inc(consts, 1)
                nc.vector.memset(neg_half[:, :], -0.5).then_inc(consts, 1)
                dve.wait_ge(weights_in, 16 * nweights)
                nc.vector.tensor_copy(id16[:, :], id32[:, :]).then_inc(consts, 1)
                dve.sem_inc(a_qk, FREE)
                dve.sem_inc(a_rest, FREE)

                def statistics(t, p):
                    nc.vector.bn_stats(stats[:, p, :], xs[:, t, :]).then_inc(a_norm, 1)
                    dve.wait_ge(a_norm, 2 * t + 1)
                    dve.sem_inc(apart, 1)
                    nc.vector.bn_aggr(moments[:, p, :], stats[:, p, :]).then_inc(a_norm, 1)
                    dve.wait_ge(a_norm, 2 * t + 2)
                    nc.vector.tensor_scalar(var_eps[:, p:p + 1], moments[:, p, 1:2], EPS, None,
                                            ALU.add).then_inc(a_var, 1)

                def norm(t, p):
                    dve.wait_ge(a_rstd, t + 1)
                    dve.wait_ge(a_xt, FREE + t - 1)
                    nc.vector.tensor_scalar(xhat[:, p, :], xs[:, t, :], moments[:, p, 0:1],
                                            rstd[:, p:p + 1], ALU.subtract, ALU.mult).then_inc(a_xhat, 1)

                def step(b, u):
                    t = TPB * b + u
                    p = u % 2
                    if exists(t + 2):
                        norm(t + 2, p)
                    if exists(t + 3):
                        if u % HALF == 1:
                            dve.wait_ge(x_in, 16 * (2 * b + u // HALF + 2))
                        statistics(t + 3, 1 - p)
                    if exists(t + 1):
                        dve.wait_ge(a_proj, FREE + t + 2)
                        dve.wait_ge(a_roped, FREE + t)
                        nc.vector.tensor_copy(qk[:, 1 - p, :], ps[:, bank_qk + 1 - p, 0:QK]).then_inc(a_qk, 1)
                    if exists(t):
                        par, cols = u // HALF, slice(u % HALF * P, (u % HALF + 1) * P)
                        dve.wait_ge(a_part0, FREE + t + 1)
                        nc.vector.tensor_tensor(rest[:, p], qk_t[:, p], parts[:, par, 0, :, cols],
                                                ALU.subtract).then_inc(a_rest, 1)
                        dve.wait_ge(a_rest, FREE + t + 1)
                        nc.vector.tensor_copy(parts[:, par, 1, :, cols], rest[:, p]).then_inc(a_part1, 1)
                        dve.wait_ge(a_part1, t + 1)
                        nc.vector.tensor_tensor(parts[:, par, 2, :, cols], rest[:, p],
                                                parts[:, par, 1, :, cols],
                                                ALU.subtract).then_inc(a_split, 1)

                pipelined(dve, step, 3)

            @block.scalar
            def _(act):
                nc.scalar.preload_act_table_set("natural_log_exp_and_others")

                def load(dst, src):
                    act.dma_start(dst, src).then_inc(weights_in, 16)

                load(id32[:, :], ident)
                load(wa[:, :, :], w_attn.rearrange("(c p) n -> p c n", p=P))
                load(rope_sb[:, :, :, :], rope)
                load(bo_row[:, :], b_out.partition_broadcast(P))
                load(br_row[:, :], b_router.partition_broadcast(P))
                load(before_sb[:, :], before)
                for c in range(DC):
                    rows = slice(c * P, (c + 1) * P)
                    load(wf[:, c, 0:D], w_base[rows, :])
                    load(wf[:, c, D + R:D + NLR].rearrange("p (e r) -> p e r", r=R),
                         a_r[:, rows, :].rearrange("e p r -> p e r"))
                load(wf[:, :, D:D + R], a_s.rearrange("(c p) r -> p c r", p=P))
                load(wf[:, :, D + NLR:NF], w_router.rearrange("(c p) e -> p c e", p=P))
                load(wlr[0:R, :], b_s)
                load(wlr[R:NLR, :], b_r.rearrange("e r d -> (e r) d"))
                act.dma_start(wlr[NLR:NLR + 1, :], b_base.unsqueeze(0)).then_inc(consts, 16)
                act.sem_inc(a_xts, FREE)
                act.sem_inc(a_v, FREE)
                act.sem_inc(a_part0, FREE)
                for e in range(2):
                    act.sem_inc(a_stored[e], 1)
                act.wait_ge(consts, 23)

                def step(b, u):
                    t = TPB * b + u
                    p = u % 2
                    if exists(t + 2):
                        act.wait_ge(a_xt, FREE + t + 3)
                        act.wait_ge(a_proj, FREE + t + 1)
                        nc.scalar.copy(xhat_t[:, p].rearrange("p c n -> p (c n)"),
                                       ps[:, bank_xt + p, 0:D]).then_inc(a_xts, 1)
                    if exists(t + 1):
                        v = (u + 1) % TPB
                        vpar, vu = v // HALF, v % HALF
                        act.wait_ge(a_proj, FREE + t + 2)
                        if v % HALF == 0:
                            act.wait_ge(a_stored[vpar], 1 + 16 * nstores * (b if v else b + (u + 1) // TPB))
                        nc.scalar.copy(v_out[:, vpar].rearrange("p g (n e) -> p g n e", e=DV)[:, :, vu, :],
                                       ps[:, bank_v + 1 - p, 0:D].rearrange("p (g e) -> p g e", e=DV)
                                       ).then_inc(a_v, 1)
                    if exists(t):
                        par, cols = u // HALF, slice(u % HALF * P, (u % HALF + 1) * P)
                        act.wait_ge(a_qkt, FREE + t + 1)
                        act.wait_ge(a_rest, FREE + t - 1)
                        bank = ps[:, bank_qkt + p, 0:(DC + 1) * P].rearrange("p (c n) -> p c n", n=P)
                        nc.scalar.mul(qk_t[:, p, 0:DC, :], bank[:, 0:DC, :], SCALE).then_inc(a_qkts, 1)
                        nc.scalar.copy(qk_t[0:KV * DK, p, DC, :], bank[0:KV * DK, DC, :]).then_inc(a_qkts, 1)
                        act.wait_ge(a_qkts, 2 * (t + 1))
                        if u % HALF == 0:
                            act.wait_ge(a_stored[par], 1 + 16 * nstores * b)
                        nc.scalar.copy(parts[:, par, 0, :, cols], qk_t[:, p]).then_inc(a_part0, 1)

                pipelined(act, step, 2)

            @block.tensor
            def _(pe):
                pe.sem_inc(a_xt, FREE)
                pe.sem_inc(a_proj, FREE)
                pe.sem_inc(a_qkt, FREE)
                pe.wait_ge(weights_in, 16 * nweights)

                def step(b, u):
                    t = TPB * b + u
                    p = u % 2
                    if exists(t + 2):
                        pe.wait_ge(a_xhat, t + 3)
                        pe.wait_ge(a_xts, FREE + t + 1)
                        for c in range(DC):
                            mm = nc.tensor.transpose(ps[:, bank_xt + p, c * P:(c + 1) * P],
                                                     xhat[:, p, c * P:(c + 1) * P], id32[:, :])
                        mm.then_inc(a_xt, 1)
                    if exists(t + 1):
                        pe.wait_ge(a_xts, FREE + t + 2)
                        pe.wait_ge(a_qk, FREE + t)
                        pe.wait_ge(a_v, FREE + t)
                        for bank, lo, hi in ((bank_qk, 0, QK), (bank_v, QK, QKV)):
                            for c in range(DC):
                                mm = nc.tensor.matmul(ps[:, bank + 1 - p, 0:hi - lo], xhat_t[:, 1 - p, c, :],
                                                      wa[:, c, lo:hi], start=(c == 0), stop=(c == DC - 1))
                        mm.then_inc(a_proj, 1)
                    if exists(t):
                        pe.wait_ge(a_roped, FREE + t + 1)
                        pe.wait_ge(a_part0, FREE + t - 1)
                        for c in range(DC + 1):
                            n = min(P, QK - c * P)
                            mm = nc.tensor.transpose(ps[0:n, bank_qkt + p, c * P:(c + 1) * P],
                                                     qkr[:, p, c * P:c * P + n], id32[:, :])
                        mm.then_inc(a_qkt, 1)

                pipelined(pe, step, 2)

        b_loaded = [sem(f"b_loaded{e}") for e in range(2)]
        b_s1 = sem("b_s1")
        b_max = sem("b_max")
        b_exp1 = sem("b_exp1")
        b_ln = sem("b_ln")
        b_chain = sem("b_chain")
        b_parts = sem("b_parts")
        b_misc = sem("b_misc")
        b_read = sem("b_read")
        b_rows = sem("b_rows")
        b_shift = sem("b_shift")
        b_s2 = sem("b_s2")
        b_exp2 = sem("b_exp2")
        b_pv = sem("b_pv")
        b_ctx = sem("b_ctx")
        bank_s1, bank_s2, bank_ctx, bank_misc = 0, 4, 6, 7
        nchain = 4

        with nc.Block() as block:
            def body(eng, step):
                with rounds(nc, eng, GROUPS - 2, 2) as i2:
                    for e in range(2):
                        for s in range(STEPS):
                            step(i2 + e, e, s)
                for i in (GROUPS - 2, GROUPS - 1):
                    for s in range(STEPS):
                        step(i, i % 2, s)

            def last(i):
                return isinstance(i, int) and i == GROUPS - 1

            def tile_at(i, e, n):
                if last(i) and n >= STEPS:
                    return None
                return (e + n // STEPS) % 2, n % STEPS // TPB, n % TPB

            @block.sync
            def _(sp):
                def fetch(i, e):
                    b, g = i // KV, i % KV
                    done = b_loaded[e]
                    for s in range(SLOTS):
                        rows = slice(s * DK, (s + 1) * DK)
                        sp.dma_start(q3[e][rows, :, :],
                                     q_dram[b, s, bass.ts(g, HPG * DK), :].rearrange("(h d) t -> d h t", d=DK)
                                     ).then_inc(done, 16)
                        sp.dma_start(k3[e][rows, :], k_dram[b, s, bass.ts(g, DK), :]).then_inc(done, 16)
                    sp.dma_start(vg[e][:, :, :].rearrange("p k e -> p (k e)"), v_dram[b, g, :, :]).then_inc(done, 16)
                    sp.dma_start(wo[e][:, :, :],
                                 w_out[bass.ts(g, HPG * DV), :].rearrange("(q p) n -> p q n", p=P)
                                 ).then_inc(done, 16)

                def put_shift(i, e, pair):
                    sp.wait_ge(b_rows, 2 * i + pair + 1)
                    sp.sem_inc(apart, 1)
                    for h in range(2):
                        sp.dma_start(q3[e][KS:KS + NSH, 2 * pair + h, :],
                                     shift_rows[pair][h * NSH:(h + 1) * NSH, :]).then_inc(b_shift, 16)

                def group(i, e):
                    put_shift(i, e, 1)
                    if not last(i):
                        put_shift(i + 1, 1 - e, 0)
                    if not isinstance(i, int):
                        sp.wait_ge(b_misc, 1 + NMISC * (i + 1))
                        sp.sem_inc(apart, 1)
                        fetch(i + 2, e)

                fetch(0, 0)
                fetch(1, 1)
                put_shift(0, 0, 0)
                with rounds(nc, sp, GROUPS - 2, 2) as i2:
                    for e in range(2):
                        group(i2 + e, e)
                group(GROUPS - 2, 0)
                group(GROUPS - 1, 1)

            @block.tensor
            def _(pe):
                pe.sem_inc(b_pv, RING)

                def scores_max(j, e, h, qt):
                    pair_bank = bank_s1 + 2 * (qt % 2)
                    pe.wait_ge(b_exp1, FREE + j - 1)
                    for k in range(2):
                        mm = nc.tensor.matmul(ps[:, pair_bank + k, :], q3[e][0:KS, h, qt * P:(qt + 1) * P],
                                              k3[e][0:KS, k * HT:(k + 1) * HT], start=True, stop=True)
                    mm.then_inc(b_s1, 1)

                def shift_rows_t(unit, use, pair):
                    pe.wait_ge(b_parts, unit + 1)
                    pe.wait_ge(b_read, use)
                    rows = ps[0:2 * NSH, bank_misc, :].bitcast(BF16)
                    for qt in range(TPB):
                        mm = nc.tensor.transpose(rows[:, qt * P:(qt + 1) * P],
                                                 shift_parts[:, qt].rearrange("p h k -> p (h k)"), id16[:, :])
                    mm.then_inc(b_misc, 1)

                def scores(i, e, s):
                    pair, qh, kt = s // 16, s // TPB % 2, s % TPB
                    pe.wait_ge(b_exp2, STEPS * i + s)
                    if s % 16 == 0:
                        pe.wait_ge(b_shift, 32 * (2 * i + pair + 1))
                    for h in range(2):
                        mm = nc.tensor.matmul(ps[:, bank_s2 + h, :], k3[e][0:KS + NSH, kt * P:(kt + 1) * P],
                                              q3[e][0:KS + NSH, 2 * pair + h, qh * HT:(qh + 1) * HT],
                                              start=True, stop=True)
                    mm.then_inc(b_s2, 1)

                def context(i, e, s):
                    kt = s % TPB
                    pe.wait_ge(b_exp2, STEPS * i + s + 1)
                    if kt == 0:
                        pe.wait_ge(b_ctx, 1 + 4 * i + s // TPB)
                    for h in range(2):
                        mm = nc.tensor.matmul(ps[h * DV:(h + 1) * DV, bank_ctx, :], vg[e][:, kt, :],
                                              probs[:, s % RING, h, :], start=(kt == 0), stop=(kt == TPB - 1))
                    mm.then_inc(b_pv, 1)

                def project(i, e, use, qt):
                    pe.wait_ge(b_ctx, 1 + 4 * i + 3 + qt // HALF)
                    pe.wait_ge(b_read, use)
                    for k in range(2):
                        for pair in range(2):
                            mm = nc.tensor.matmul(ps[:, bank_misc, k * D:(k + 1) * D],
                                                  ctx_t[:, pair, (qt + k) * P:(qt + k + 1) * P],
                                                  wo[e][:, pair, :], start=(pair == 0), stop=(pair == 1))
                    mm.then_inc(b_misc, 1)

                def step(i, e, s):
                    use = 1 + NMISC * i
                    ahead = tile_at(i, e, s + LEAD)
                    if ahead is not None:
                        if s == STEPS - LEAD:
                            pe.wait_ge(b_loaded[1 - e], 16 * NFETCH * ((i + 1) // 2 + 1))
                        scores_max(STEPS * i + s + LEAD, *ahead)
                    if s < STEPS - 1:
                        scores(i, e, s + 1)
                    elif not last(i):
                        scores(i + 1, 1 - e, 0)
                    context(i, e, s)
                    if s == 12:
                        shift_rows_t(2 * i + 1, use, 1)
                    if s == 24:
                        project(i, e, use + 1, 0)
                    if s == 25:
                        project(i, e, use + 2, 2)
                    if s == 28 and not last(i):
                        shift_rows_t(2 * i + 2, use + 3, 0)
                    if s == 31:
                        gone = 1 if last(i) else 0
                        project(i, e, use + 4 - gone, 4)
                        project(i, e, use + 5 - gone, 6)

                pe.wait_ge(b_loaded[0], 16 * NFETCH)
                for j in range(LEAD):
                    scores_max(j, 0, j // TPB, j % TPB)
                    if j == 20:
                        shift_rows_t(0, 0, 0)
                scores(0, 0, 0)
                body(pe, step)

            @block.scalar
            def _(act):
                act.sem_inc(b_exp1, FREE)

                def sum_exp(j, e, h, qt):
                    pair_bank = bank_s1 + 2 * (qt % 2)
                    tile = ps[:, pair_bank:pair_bank + 2, :]
                    pair, col = h // 2, h % 2 * TPB + qt
                    act.wait_ge(b_max, j + 1)
                    nc.scalar.activation(tile, tile, ACT.Exp, bias=negm[:, pair, col:col + 1],
                                         accum_out=den[:, pair, col:col + 1]).then_inc(b_exp1, 1)

                def log_sum(unit, pair, j):
                    act.wait_ge(b_exp1, FREE + j + 1)
                    nc.scalar.activation(lnden[:, pair, :], den[:, pair, :], ACT.Ln).then_inc(b_ln, 1)

                def probabilities(i, s):
                    n = STEPS * i + s
                    act.wait_ge(b_s2, n + 1)
                    act.wait_ge(b_pv, n + 1)
                    nc.scalar.activation(probs[:, s % RING, :, :], ps[:, bank_s2:bank_s2 + 2, :],
                                         ACT.Exp).then_inc(b_exp2, 1)

                def step(i, e, s):
                    probabilities(i, s)
                    ahead = tile_at(i, e, s + LEAD - 1)
                    if ahead is not None:
                        sum_exp(STEPS * i + s + LEAD - 1, *ahead)
                    if s == 9:
                        log_sum(2 * i + 1, 1, STEPS * i + 31)
                    if s == 25 and not last(i):
                        log_sum(2 * i + 2, 0, STEPS * i + 47)

                for j in range(LEAD - 1):
                    sum_exp(j, 0, j // TPB, j % TPB)
                    if j == 16:
                        log_sum(0, 0, 15)
                body(act, step)

            @block.vector
            def _(dve):
                dve.sem_inc(b_ctx, 1)

                def row_max(j, e, h, qt):
                    pair_bank = bank_s1 + 2 * (qt % 2)
                    pair, col = h // 2, h % 2 * TPB + qt
                    dve.wait_ge(b_s1, j + 1)
                    nc.vector.tensor_reduce(negm[:, pair, col:col + 1], ps[:, pair_bank:pair_bank + 2, :],
                                            AX.XY, ALU.max, negate=True).then_inc(b_max, 1)

                def split_shift(unit, pair):
                    done = nchain * unit
                    out_part = [shift_parts[:, :, :, k].rearrange("p t h -> p h t") for k in range(NSH)]
                    by_head = [a[:, :].rearrange("p (h t) -> p h t", h=2) for a in (shift, shift_rest)]
                    dve.wait_ge(b_ln, unit + 1)
                    nc.vector.tensor_tensor(shift[:, :], negm[:, pair, :], lnden[:, pair, :],
                                            ALU.subtract).then_inc(b_chain, 1)
                    dve.wait_ge(b_chain, done + 1)
                    nc.vector.tensor_copy(out_part[0], by_head[0]).then_inc(b_chain, 1)
                    dve.wait_ge(b_chain, done + 2)
                    nc.vector.tensor_tensor(by_head[1], by_head[0], out_part[0], ALU.subtract).then_inc(b_chain, 1)
                    dve.wait_ge(b_chain, done + 3)
                    nc.vector.tensor_copy(out_part[1], by_head[1]).then_inc(b_chain, 1)
                    dve.wait_ge(b_chain, done + 4)
                    nc.vector.tensor_tensor(out_part[2], by_head[1], out_part[1], ALU.subtract).then_inc(b_parts, 1)

                def copy_rows(unit, use, pair):
                    dve.wait_ge(b_misc, use + 1)
                    nc.vector.tensor_copy(shift_rows[pair][:, :],
                                          ps[0:2 * NSH, bank_misc, :].bitcast(BF16)).then_inc(b_read, 1)
                    dve.wait_ge(b_read, use + 1)
                    dve.sem_inc(b_rows, 1)

                def keep_context(i, s):
                    pair, qh = s // 16, s // TPB % 2
                    dve.wait_ge(b_pv, RING + STEPS * i + s + 1)
                    nc.vector.tensor_copy(ctx_t[:, pair, qh * HT:(qh + 1) * HT],
                                          ps[:, bank_ctx, :]).then_inc(b_ctx, 1)

                def add_output(i, use, qt):
                    dve.wait_ge(b_misc, use + 1)
                    rows = xs[:, bass.ds(i // KV * TPB + qt, 2), :]
                    nc.vector.tensor_tensor(rows, rows, ps[:, bank_misc, :].rearrange("p (k d) -> p k d", k=2),
                                            ALU.add).then_inc(b_read, 1)

                def step(i, e, s):
                    use = 1 + NMISC * i
                    ahead = tile_at(i, e, s + LEAD)
                    if ahead is not None:
                        row_max(STEPS * i + s + LEAD, *ahead)
                    if s == 10:
                        split_shift(2 * i + 1, 1)
                    if s == 12:
                        copy_rows(2 * i + 1, use, 1)
                    if s % TPB == TPB - 1:
                        keep_context(i, s)
                    if s == 24:
                        add_output(i, use + 1, 0)
                    if s == 25:
                        add_output(i, use + 2, 2)
                    if s == 26 and not last(i):
                        split_shift(2 * i + 2, 0)
                    if s == 28 and not last(i):
                        copy_rows(2 * i + 2, use + 3, 0)
                    if s == 31:
                        gone = 1 if last(i) else 0
                        add_output(i, use + 4 - gone, 4)
                        add_output(i, use + 5 - gone, 6)

                for j in range(LEAD):
                    row_max(j, 0, j // TPB, j % TPB)
                    if j == 18:
                        split_shift(0, 0)
                    if j == 20:
                        copy_rows(0, 0, 0)
                body(dve, step)

        c_norm = sem("c_norm")
        c_var = sem("c_var")
        c_rstd = sem("c_rstd")
        c_xhat = sem("c_xhat")
        c_xt = sem("c_xt")
        c_xts = sem("c_xts")
        c_ff = sem("c_ff")
        c_gate = sem("c_gate")
        c_shifted = sem("c_shifted")
        c_exp = sem("c_exp")
        c_wexp = sem("c_wexp")
        c_hw = sem("c_hw")
        c_ht = sem("c_ht")
        c_hts = sem("c_hts")
        c_out = sem("c_out")
        c_y = sem("c_y")
        c_stored = [sem(f"c_stored{q}") for q in range(2)]
        bank_ff, bank_cxt, bank_ht = 0, 4, 6
        ngate = 10

        with nc.Block() as block:
            def idle(k, q):
                pass

            def sets(eng, first, front, back):
                first(0, 0)
                front(0, 0)
                first(1, 1)
                with rounds(nc, eng, SETS - 2, 2) as k2:
                    for q in range(2):
                        front(k2 + q + 1, 1 - q)
                        first(k2 + q + 2, q)
                        back(k2 + q, q)
                front(SETS - 1, 1)
                back(SETS - 2, 0)
                back(SETS - 1, 1)

            @block.sync
            def _(sp):
                for q in range(2):
                    sp.sem_inc(c_stored[q], 1)
                with rounds(nc, sp, SETS, 2) as k2:
                    for q in range(2):
                        k = k2 + q
                        sp.wait_ge(c_y, FREE + k + 1)
                        sp.sem_inc(apart, 1)
                        sp.dma_start(out_t[:, bass.ts(k, FSET), :], y[:, q]).then_inc(c_stored[q], 16)
                for q in range(2):
                    sp.wait_ge(c_stored[q], 1 + 16 * SETS // 2)

            @block.gpsimd
            def _(pool):
                def inverse_root(k, q):
                    slots = slice(FSET * q, FSET * (q + 1))
                    pool.wait_ge(c_var, k + 1)
                    nc.gpsimd.tensor_tensor(rstd[:, slots], var_eps[:, slots], neg_half[:, :],
                                            ALU.pow).then_inc(c_rstd, 1)

                sets(pool, inverse_root, idle, idle)

            @block.vector
            def _(dve):
                dve.sem_inc(c_y, FREE)

                def statistics(k, q):
                    slots = slice(FSET * q, FSET * (q + 1))
                    for u in range(FSET):
                        nc.vector.bn_stats(stats[:, FSET * q + u, :], xs[:, FSET * k + u, :]).then_inc(c_norm, 1)
                    for u in range(FSET):
                        dve.wait_ge(c_norm, 2 * FSET * k + FSET + u)
                        dve.sem_inc(apart, 1)
                        nc.vector.bn_aggr(moments[:, FSET * q + u, :],
                                          stats[:, FSET * q + u, :]).then_inc(c_norm, 1)
                    dve.wait_ge(c_norm, 2 * FSET * (k + 1))
                    nc.vector.tensor_scalar(var_eps[:, slots], moments[:, slots, 1], EPS, None,
                                            ALU.add).then_inc(c_var, 1)

                def front(k, q):
                    dve.wait_ge(c_rstd, k + 1)
                    for u in range(FSET):
                        t, slot = FSET * k + u, FSET * q + u
                        dve.wait_ge(c_xt, FREE + t - 1)
                        nc.vector.tensor_scalar(xhat[:, u, :], xs[:, t, :], moments[:, slot, 0:1],
                                                rstd[:, slot:slot + 1], ALU.subtract,
                                                ALU.mult).then_inc(c_xhat, 1)

                def back(k, q):
                    ff = ps[:, bank_ff + FSET * q:bank_ff + FSET * (q + 1), :]
                    h_shared, h_routed = ff[:, :, D:D + R], ff[:, :, D + R:D + NLR]
                    wide = [P, FSET, E]
                    done = ngate * k
                    dve.wait_ge(c_ff, FREE + FSET * (k + 1))
                    nc.vector.tensor_tensor(lg[:, q], ff[:, :, D + NLR:NF],
                                            br_row[:, :].unsqueeze(1).to_broadcast(wide), ALU.add).then_inc(c_gate, 1)
                    dve.wait_ge(c_gate, done + 1)
                    nc.vector.tensor_reduce(lmax[:, q], lg[:, q], AX.X, ALU.max).then_inc(c_gate, 1)
                    dve.wait_ge(c_gate, done + 2)
                    nc.vector.tensor_tensor(lexp[:, q], lg[:, q], lmax[:, q].unsqueeze(2).to_broadcast(wide),
                                            ALU.subtract).then_inc(c_shifted, 1)
                    dve.wait_ge(c_exp, k + 1)
                    nc.vector.tensor_reduce(lsum[:, q], lexp[:, q], AX.X, ALU.add).then_inc(c_gate, 1)
                    dve.wait_ge(c_gate, done + 3)
                    nc.vector.reciprocal(linv[:, q], lsum[:, q]).then_inc(c_gate, 1)
                    dve.wait_ge(c_gate, done + 4)
                    nc.vector.tensor_tensor(gates[:, q], lexp[:, q],
                                            linv[:, q].unsqueeze(2).to_broadcast(wide), ALU.mult).then_inc(c_gate, 1)
                    dve.wait_ge(c_gate, done + 5)
                    own = gates[:, q].rearrange("p f e -> p (f e)").unsqueeze(2).to_broadcast([P, FSET * E, E])
                    for f in range(FSET):
                        rows = slice(f * E, (f + 1) * E)
                        other = gates[:, q, f:f + 1, :].to_broadcast([P, E, E])
                        nc.vector.tensor_tensor(cge[:, q, rows, :], other, own[:, rows, :], ALU.is_ge)
                        last_cmp = nc.vector.tensor_tensor(cgt[:, q, rows, :], other, own[:, rows, :], ALU.is_gt)
                    last_cmp.then_inc(c_gate, 1)
                    dve.wait_ge(c_gate, done + 6)
                    nc.vector.tensor_tensor(cge[:, q], cge[:, q], cgt[:, q], ALU.subtract).then_inc(c_gate, 1)
                    dve.wait_ge(c_gate, done + 7)
                    tie = before_sb[:, :].rearrange("p (e j) -> p e j", j=E)
                    for f in range(FSET):
                        rows = slice(f * E, (f + 1) * E)
                        last_cmp = nc.vector.tensor_tensor(cge[:, q, rows, :], cge[:, q, rows, :], tie, ALU.mult)
                    last_cmp.then_inc(c_gate, 1)
                    dve.wait_ge(c_gate, done + 8)
                    nc.vector.tensor_tensor(cgt[:, q], cgt[:, q], cge[:, q], ALU.add).then_inc(c_gate, 1)
                    dve.wait_ge(c_gate, done + 9)
                    nc.vector.tensor_reduce(rank[:, q].rearrange("p f e -> p (f e)"), cgt[:, q], AX.X, ALU.add).then_inc(c_gate, 1)
                    dve.wait_ge(c_gate, done + 10)
                    nc.vector.scalar_tensor_tensor(out=wexp[:, q], in0=rank[:, q], scalar=float(TOP_K),
                                                   in1=gates[:, q], op0=ALU.is_lt,
                                                   op1=ALU.mult).then_inc(c_wexp, 1)
                    dve.wait_ge(c_ht, FREE + k - 1)
                    nc.vector.tensor_copy(hw[:, q, :, 0:R], h_shared).then_inc(c_hw, 1)
                    dve.wait_ge(c_wexp, k + 1)
                    for f in range(FSET):
                        last_hw = nc.vector.tensor_tensor(
                            hw[:, q, f, R:NLR].rearrange("p (e r) -> p e r", r=R),
                            h_routed[:, f, :].rearrange("p (e r) -> p e r", r=R),
                            wexp[:, q, f, :].unsqueeze(2).to_broadcast([P, E, R]), ALU.mult)
                        last_hw.then_inc(c_hw, 1)
                    dve.wait_ge(c_out, FREE + k + 1)
                    dve.wait_ge(c_stored[q], 1 + 16 * (k // 2))
                    nc.vector.tensor_tensor(y[:, q], xs[:, bass.ts(k, FSET), :], ff[:, :, 0:D],
                                            ALU.add).then_inc(c_y, 1)

                sets(dve, statistics, front, back)

            @block.scalar
            def _(act):
                act.sem_inc(c_xts, FREE)
                act.sem_inc(c_hts, FREE)

                def front(k, q):
                    for u in range(FSET):
                        t = FSET * k + u
                        act.wait_ge(c_xt, FREE + t + 1)
                        act.wait_ge(c_ff, FREE + t - 1)
                        nc.scalar.copy(xhat_t[:, u].rearrange("p c n -> p (c n)"),
                                       ps[:, bank_cxt + u, 0:D]).then_inc(c_xts, 1)

                def back(k, q):
                    act.wait_ge(c_shifted, k + 1)
                    nc.scalar.activation(lexp[:, q], lexp[:, q], ACT.Exp).then_inc(c_exp, 1)
                    act.wait_ge(c_ht, FREE + k + 1)
                    act.wait_ge(c_out, FREE + k - 1)
                    nc.scalar.copy(hw_t[:, q].rearrange("p f n -> p (f n)"),
                                   ps[0:NLR + 1, bank_ht + q, 0:FSET * P]).then_inc(c_hts, 1)

                sets(act, idle, front, back)

            @block.tensor
            def _(pe):
                pe.sem_inc(c_xt, FREE)
                pe.sem_inc(c_ff, FREE)
                pe.sem_inc(c_ht, FREE)
                pe.sem_inc(c_out, FREE)

                def front(k, q):
                    pe.wait_ge(c_y, FREE + k - 1)
                    for u in range(FSET):
                        t = FSET * k + u
                        pe.wait_ge(c_xhat, t + 1)
                        pe.wait_ge(c_xts, FREE + t - 1)
                        for c in range(DC):
                            mm = nc.tensor.transpose(ps[:, bank_cxt + u, c * P:(c + 1) * P],
                                                     xhat[:, u, c * P:(c + 1) * P], id32[:, :])
                        mm.then_inc(c_xt, 1)
                    for u in range(FSET):
                        t = FSET * k + u
                        pe.wait_ge(c_xts, FREE + t + 1)
                        for c in range(DC):
                            mm = nc.tensor.matmul(ps[:, bank_ff + FSET * q + u, 0:NF], xhat_t[:, u, c, :],
                                                  wf[:, c, :], start=(c == 0), stop=(c == DC - 1))
                        mm.then_inc(c_ff, 1)

                def back(k, q):
                    pe.wait_ge(c_hw, (FSET + 1) * (k + 1))
                    pe.wait_ge(c_hts, FREE + k - 1)
                    for f in range(FSET):
                        mm = nc.tensor.transpose(ps[0:NLR + 1, bank_ht + q, f * P:(f + 1) * P],
                                                 hw[:, q, f, :], id32[:, :])
                    mm.then_inc(c_ht, 1)
                    pe.wait_ge(c_hts, FREE + k + 1)
                    for f in range(FSET):
                        mm = nc.tensor.matmul(ps[:, bank_ff + FSET * q + f, 0:D], hw_t[:, q, f, :],
                                              wlr[:, :], start=False, stop=True, skip_group_check=True)
                    mm.then_inc(c_out, 1)

                sets(pe, idle, front, back)


_INS = ['L0_attn_x', 'L0_attn_W_attn', 'L0_attn_W_out', 'L0_attn_b_out', 'L0_ffn_W_base', 'L0_ffn_b_base',
        'L0_ffn_A_s', 'L0_ffn_B_s', 'L0_ffn_A_r', 'L0_ffn_B_r', 'L0_ffn_W_router', 'L0_ffn_b_router']


def kernel(**inputs):
    import numpy as _np
    import concourse.bacc as _bacc
    from concourse import mybir as _mybir
    from concourse.bass_utils import run_bass_kernel_spmd as _run

    f32 = _np.float32
    inv_freq = (f32(1.0) / _np.power(f32(10000.0), _np.arange(0, DK, 2, dtype=f32) / f32(DK))).astype(f32)
    ang = _np.arange(L, dtype=f32)[:, None] * inv_freq[None, :]
    cos, sin = _np.cos(ang), _np.sin(ang)
    table = _np.stack([_np.concatenate([cos, cos], 1), _np.concatenate([-sin, sin], 1)], 1)
    table = _np.ascontiguousarray(table.reshape(TPB, P, 2, DK).transpose(1, 0, 2, 3)).astype(f32)
    before = _np.broadcast_to(_np.tril(_np.ones((E, E), f32), -1).reshape(1, E * E), (P, E * E))
    consts = {"rope": table, "ident": _np.eye(P, dtype=f32), "before": _np.ascontiguousarray(before)}

    nc = _bacc.Bacc("TRN2", target_bir_lowering=False, num_devices=1)
    arrays, args = {}, []
    for name, a in [(n, _np.ascontiguousarray(inputs[n])) for n in _INS] + list(consts.items()):
        arrays[f"in_{name}_dram"] = a
        args.append(nc.dram_tensor(f"in_{name}_dram", a.shape, _mybir.dt.from_np(a.dtype), kind="ExternalInput").ap())
    args.append(nc.dram_tensor("out_0_dram", (B, L, D), F32, kind="ExternalOutput").ap())
    layer_kernel(nc, *args)
    r = _run(nc, [arrays], core_ids=[0])
    return r.results[0]["out_0_dram"]
```

```python
from contextlib import ExitStack, contextmanager

import concourse.bass as bass
from concourse import mybir

F32 = mybir.dt.float32
BF16 = mybir.dt.bfloat16
ALU = mybir.AluOpType
ACT = mybir.ActivationFunctionType
AX = mybir.AxisListType

P = 128
B, L, D = 4, 1024, 256
HEADS, KV = 16, 4
HPG = HEADS // KV
DK, DV = D // HEADS, D // KV
QK = HEADS * DK + KV * DK
QKV = QK + KV * DV
DC = D // P
TILES = B * L // P
TPB = L // P
HALF = TPB // 2
HT = HALF * P
GROUPS = B * KV
EPS = 1e-5
SCALE = DK ** -0.5

RUNS = ((0, 3, 0, 0), (3, 2, 1, 0), (5, 1, 2, 0))
SLOTS = 6
PARTS = 3
PC = -(-PARTS * QK // P)
PC_ROWS = PARTS * QK - (PC - 1) * P
KS = SLOTS * DK
NSH = 3

E, R, TOP_K = 6, 16, 2
NLR = R + E * R
NF = D + NLR + E
STEPS = 2 * 2 * TPB
LEAD = 24
RING = 8
NFETCH = 2 * len(RUNS) + 1
NMISC = 10
FSET = 2
SETS = TILES // FSET
FREE = 2


@contextmanager
def rounds(nc, eng, end, step, start=0):
    with eng.Fori(start, end, step) as i:
        yield nc.s_assert_within(i, start, end - step,
                                 skip_runtime_bounds_check_because="step divides end")


def layer_kernel(nc, x, w_attn, w_out, b_out, w_base, b_base, a_s, b_s, a_r, b_r,
                 w_router, b_router, rope, ident, before, out):
    x_t = x.rearrange("b (t p) d -> p (b t) d", p=P)
    out_t = out.rearrange("b (t p) d -> p (b t) d", p=P)

    with ExitStack() as ctx:
        def sb(name, shape, dt=F32):
            return ctx.enter_context(nc.sbuf_tensor(name, shape, dt))

        def sem(name):
            return ctx.enter_context(nc.semaphore(name))

        qk_dram = nc.dram_tensor("qk_parts", [B, PARTS * QK, L], BF16).ap()
        v_dram = nc.dram_tensor("v_rows", [B, KV, P, TPB * DV], F32).ap()

        xs = sb("xs", [P, TILES, D])
        wa = sb("wa", [P, DC, QKV])
        wf = sb("wf", [P, DC, NF])
        wlr = sb("wlr", [NLR + 1, D])
        bo_row = sb("bo_row", [P, D])
        br_row = sb("br_row", [P, E])
        rope_sb = sb("rope_sb", [P, TPB, 2, DK])
        id32 = sb("id32", [P, P])
        id16 = sb("id16", [P, P], BF16)
        before_sb = sb("before_sb", [P, E * E])

        stats = sb("stats", [P, 4, 6])
        moments = sb("moments", [P, 4, 2])
        var_eps = sb("var_eps", [P, 4])
        rstd = sb("rstd", [P, 4])
        neg_half = sb("neg_half", [P, 2])
        xhat = sb("xhat", [P, 2, D])
        xhat_t = sb("xhat_t", [P, 2, DC, P])

        qk = sb("qk", [P, 2, QK])
        rope_c = sb("rope_c", [P, 2, QK])
        rope_s = sb("rope_s", [P, 2, QK])
        qkr = sb("qkr", [P, QK])
        rest = sb("rest", [P, QK])
        parts = sb("parts", [P, 2, PARTS * QK], BF16)
        parts_t = sb("parts_t", [P, 2, PC, HT], BF16)
        v_out = sb("v_out", [P, 2, KV, HALF * DV])

        q3 = [sb(f"q3_{e}", [P, HPG, L], BF16) for e in range(2)]
        k3 = [sb(f"k3_{e}", [P, L], BF16) for e in range(2)]
        vg = [sb(f"vg_{e}", [P, TPB, DV]) for e in range(2)]
        wo = [sb(f"wo_{e}", [P, 2, D]) for e in range(2)]
        probs = sb("probs", [P, RING, 2, HT])
        negm = sb("negm", [P, 2, 2 * TPB])
        den = sb("den", [P, 2, 2 * TPB])
        lnden = sb("lnden", [P, 2, 2 * TPB])
        shift = sb("shift", [P, 2 * TPB])
        shift_rest = sb("shift_rest", [P, 2 * TPB])
        shift_parts = sb("shift_parts", [P, TPB, 2, NSH], BF16)
        shift_rows = [sb(f"shift_rows_{q}", [2 * NSH, L], BF16) for q in range(2)]
        ctx_t = sb("ctx_t", [P, 2, L])

        lg = sb("lg", [P, 2, FSET, E])
        lmax = sb("lmax", [P, 2, FSET])
        lexp = sb("lexp", [P, 2, FSET, E])
        lsum = sb("lsum", [P, 2, FSET])
        linv = sb("linv", [P, 2, FSET])
        gates = sb("gates", [P, 2, FSET, E])
        cge = sb("cge", [P, 2, FSET * E, E])
        cgt = sb("cgt", [P, 2, FSET * E, E])
        rank = sb("rank", [P, 2, FSET, E])
        wexp = sb("wexp", [P, 2, FSET, E])
        hw = sb("hw", [P, 2, FSET, NLR + 1])
        hw_t = sb("hw_t", [NLR + 1, 2, FSET, P])
        y = sb("y", [P, 2, FSET, D])

        apart = sem("apart")
        ps = ctx.enter_context(nc.psum_tensor("ps", [P, 8, 512], F32))

        first_in = sem("first_in")
        weights_in = sem("weights_in")
        x_in = [sem(f"x_in{e}") for e in range(2)]
        consts = sem("consts")
        a_scaled = sem("a_scaled")
        a_norm = sem("a_norm")
        a_var = sem("a_var")
        a_rstd = sem("a_rstd")
        a_xhat = sem("a_xhat")
        a_xt = sem("a_xt")
        a_xts = sem("a_xts")
        a_proj = sem("a_proj")
        a_qk = sem("a_qk")
        a_v = sem("a_v")
        a_rope = sem("a_rope")
        a_roped = sem("a_roped")
        a_part0 = sem("a_part0")
        a_rest = sem("a_rest")
        a_part1 = sem("a_part1")
        a_split = sem("a_split")
        a_partt = sem("a_partt")
        a_kept = sem("a_kept")
        a_stored = [sem(f"a_stored{e}") for e in range(2)]
        b_loaded = [sem(f"b_loaded{e}") for e in range(2)]
        wo_loaded = [sem(f"wo_loaded{e}") for e in range(2)]
        nfirst = 4
        nweights = 2 + 2 * DC + 5
        nstores = 3
        bank_xt, bank_qk, bank_v, bank_pt = 0, 2, 4, 6

        def pipelined(eng, step, lead):
            for u in range(-lead, 0):
                step(0, u)
            with rounds(nc, eng, B - 1, 1) as b:
                for u in range(TPB):
                    step(b, u)
            for u in range(TPB):
                step(B - 1, u)

        def exists(t):
            return not isinstance(t, int) or 0 <= t < TILES

        def fetch(sp, i, e):
            b, g = i // KV, i % KV
            done = b_loaded[e]
            by_part = qk_dram[b].rearrange("(k r) t -> k r t", k=PARTS)
            for slot, n, qp, kp in RUNS:
                rows = slice(slot * DK, (slot + n) * DK)
                q_rows = by_part[qp:qp + 1, bass.ts(g, DK * HPG), :].rearrange("k (d h) t -> k d (h t)", h=HPG)
                k_rows = by_part[kp:kp + n, HEADS * DK:QK, :].rearrange("k (d h) t -> k d h t", h=KV)[:, :, g, :]
                sp.dma_start(q3[e][rows, :, :].rearrange("r h t -> r (h t)"),
                             q_rows.to_broadcast([n, DK, HPG * L])).then_inc(done, 16)
                sp.dma_start(k3[e][rows, :], k_rows).then_inc(done, 16)
            sp.dma_start(vg[e][:, :, :].rearrange("p k e -> p (k e)"), v_dram[b, g, :, :]).then_inc(done, 16)

        def fetch_wo(sp, i, e):
            sp.dma_start(wo[e][:, :, :],
                         w_out[bass.ts(i % KV, HPG * DV), :].rearrange("(q p) n -> p q n", p=P)
                         ).then_inc(wo_loaded[e], 16)

        with nc.Block() as block:
            @block.sync
            def _(sp):
                def load_x(hb, par):
                    sp.dma_start(xs[:, bass.ts(hb, HALF), :],
                                 x_t[:, bass.ts(hb, HALF), :]).then_inc(x_in[par], 16)

                def store(b, par):
                    hb = 2 * b + par
                    sp.wait_ge(a_kept, 2 * FREE + 2 * HALF * (hb + 1))
                    sp.sem_inc(apart, 1)
                    sp.wait_ge(a_v, FREE + HALF * (hb + 1))
                    sp.sem_inc(apart, 1)
                    cols = slice(par * HT, (par + 1) * HT)
                    full = (PC - 1) * P
                    sp.dma_start(qk_dram[b, 0:full, cols].rearrange("(c p) t -> p c t", p=P),
                                 parts_t[:, par, 0:PC - 1, :]).then_inc(a_stored[par], 16)
                    sp.dma_start(qk_dram[b, full:PARTS * QK, cols],
                                 parts_t[0:PC_ROWS, par, PC - 1, :]).then_inc(a_stored[par], 16)
                    vcols = slice(par * HALF * DV, (par + 1) * HALF * DV)
                    sp.dma_start(v_dram[b, :, :, vcols].rearrange("g p n -> p g n"),
                                 v_out[:, par, :, :]).then_inc(a_stored[par], 16)

                def half_row(b, par, last=False):
                    if not last:
                        sp.wait_ge(x_in[par], 16 * (b + 1))
                        sp.sem_inc(apart, 1)
                        load_x(2 * b + par + 2, par)
                    store(b, par)

                load_x(0, 0)
                load_x(1, 1)
                with rounds(nc, sp, B - 1, 1) as b:
                    half_row(b, 0)
                    half_row(b, 1)
                for par in range(2):
                    sp.wait_ge(a_stored[par], 1 + 16 * nstores)
                for i in range(2):
                    fetch(sp, i, i)
                fetch_wo(sp, 0, 0)
                half_row(B - 1, 0, last=True)
                half_row(B - 1, 1, last=True)

            @block.gpsimd
            def _(pool):
                pool.sem_inc(a_rope, 3 * FREE)
                pool.wait_ge(consts, 5)
                pool.wait_ge(first_in, 16 * nfirst)
                nh, half = QK // DK, DK // 2

                def rotate(t, u):
                    p = u % 2
                    xv, cv, sv = (a[:, p, :].rearrange("p (h i) -> p h i", i=DK) for a in (qk, rope_c, rope_s))

                    def table(k, lo, hi):
                        return rope_sb[:, u:u + 1, k, lo:hi].to_broadcast([P, nh, hi - lo])

                    pool.wait_ge(a_qk, FREE + t + 1)
                    pool.wait_ge(a_roped, FREE + t - 1)
                    nc.gpsimd.tensor_tensor(cv, xv, table(0, 0, DK), ALU.mult).then_inc(a_rope, 1)
                    nc.gpsimd.tensor_tensor(sv[:, :, 0:half], xv[:, :, half:DK], table(1, 0, half),
                                            ALU.mult).then_inc(a_rope, 1)
                    nc.gpsimd.tensor_tensor(sv[:, :, half:DK], xv[:, :, 0:half], table(1, half, DK),
                                            ALU.mult).then_inc(a_rope, 1)

                def step(b, u):
                    t = TPB * b + u
                    if exists(t + 2):
                        rotate(t + 2, (u + 2) % TPB)
                    if exists(t + 5):
                        pool.wait_ge(a_xhat, t + 6)
                        nc.gpsimd.tensor_tensor(xs[:, t + 5, :], xs[:, t + 5, :], bo_row[:, :], ALU.add)
                    if exists(t + 6):
                        slot = slice((u + 6) % 4, (u + 6) % 4 + 1)
                        pool.wait_ge(a_var, t + 7)
                        nc.gpsimd.tensor_tensor(rstd[:, slot], var_eps[:, slot], neg_half[:, 0:1],
                                                ALU.pow).then_inc(a_rstd, 1)

                pipelined(pool, step, 6)

            @block.vector
            def _(dve):
                for e in range(2):
                    nc.vector.memset(k3[e][KS:P, :], 1.0).then_inc(consts, 1)
                nc.vector.memset(hw[:, :, :, NLR:NLR + 1], 1.0).then_inc(consts, 1)
                nc.vector.memset(neg_half[:, :], -0.5).then_inc(consts, 1)
                dve.wait_ge(first_in, 16 * nfirst)
                nc.vector.tensor_copy(id16[:, :], id32[:, :]).then_inc(consts, 1)
                nc.vector.tensor_scalar(wa[:, :, 0:HEADS * DK], wa[:, :, 0:HEADS * DK], SCALE, None,
                                        ALU.mult).then_inc(a_scaled, 1)
                dve.sem_inc(a_roped, FREE)

                def statistics(t, p):
                    nc.vector.bn_stats(stats[:, p, :], xs[:, t, :]).then_inc(a_norm, 1)
                    dve.wait_ge(a_norm, 2 * t + 1)
                    dve.sem_inc(apart, 1)
                    nc.vector.bn_aggr(moments[:, p, :], stats[:, p, :]).then_inc(a_norm, 1)
                    dve.wait_ge(a_norm, 2 * t + 2)
                    nc.vector.tensor_scalar(var_eps[:, p:p + 1], moments[:, p, 1:2], EPS, None,
                                            ALU.add).then_inc(a_var, 1)

                def norm(t, slot, p):
                    dve.wait_ge(a_rstd, t + 1)
                    dve.wait_ge(a_xt, FREE + t - 1)
                    nc.vector.tensor_scalar(xhat[:, p, :], xs[:, t, :], moments[:, slot, 0:1],
                                            rstd[:, slot:slot + 1], ALU.subtract, ALU.mult).then_inc(a_xhat, 1)

                def split(t, p):
                    part = [parts[:, p, k * QK:(k + 1) * QK] for k in range(PARTS)]
                    dve.wait_ge(a_rope, 3 * FREE + 3 * (t + 1))
                    by_dim = qkr[:, :].rearrange("p (b i h) -> p b h i", i=DK, h=HPG)
                    c, s = (a[:, p, :].rearrange("p (b h i) -> p b h i", i=DK, h=HPG) for a in (rope_c, rope_s))
                    nc.vector.tensor_tensor(by_dim, c, s,
                                            ALU.add).then_inc(a_roped, 1)
                    dve.wait_ge(a_roped, FREE + t + 1)
                    dve.wait_ge(a_partt, FREE + t - 1)
                    nc.vector.tensor_copy(part[0], qkr[:, :]).then_inc(a_part0, 1)
                    dve.wait_ge(a_part0, t + 1)
                    nc.vector.tensor_tensor(rest[:, :], qkr[:, :], part[0], ALU.subtract).then_inc(a_rest, 1)
                    dve.wait_ge(a_rest, t + 1)
                    nc.vector.tensor_copy(part[1], rest[:, :]).then_inc(a_part1, 1)
                    dve.wait_ge(a_part1, t + 1)
                    nc.vector.tensor_tensor(part[2], rest[:, :], part[1], ALU.subtract).then_inc(a_split, 1)

                def step(b, u):
                    t = TPB * b + u
                    if exists(t + 5):
                        norm(t + 5, (u + 5) % 4, (u + 5) % 2)
                    if exists(t + 6):
                        row, v = b + (u + 6) // TPB, (u + 6) % TPB
                        if v % HALF == 0:
                            dve.wait_ge(x_in[v // HALF], 16 * (row + 1))
                        statistics(t + 6, v % 4)
                    if exists(t + 1):
                        split(t + 1, (u + 1) % 2)

                pipelined(dve, step, 6)

            @block.scalar
            def _(act):
                nc.scalar.preload_act_table_set("natural_log_exp_and_others")

                def load(dst, src, done):
                    act.dma_start(dst, src).then_inc(done, 16)

                load(wa[:, :, :], w_attn.rearrange("(c p) n -> p c n", p=P), first_in)
                load(id32[:, :], ident, first_in)
                load(rope_sb[:, :, :, :], rope, first_in)
                load(bo_row[:, :], b_out.partition_broadcast(P), first_in)
                load(br_row[:, :], b_router.partition_broadcast(P), weights_in)
                load(before_sb[:, :], before, weights_in)
                for c in range(DC):
                    rows = slice(c * P, (c + 1) * P)
                    load(wf[:, c, 0:D], w_base[rows, :], weights_in)
                    load(wf[:, c, D + R:D + NLR].rearrange("p (e r) -> p e r", r=R),
                         a_r[:, rows, :].rearrange("e p r -> p e r"), weights_in)
                load(wf[:, :, D:D + R], a_s.rearrange("(c p) r -> p c r", p=P), weights_in)
                load(wf[:, :, D + NLR:NF], w_router.rearrange("(c p) e -> p c e", p=P), weights_in)
                load(wlr[0:R, :], b_s, weights_in)
                load(wlr[R:NLR, :], b_r.rearrange("e r d -> (e r) d"), weights_in)
                act.dma_start(wlr[NLR:NLR + 1, :], b_base.unsqueeze(0)).then_inc(weights_in, 16)
                act.sem_inc(a_xts, FREE)
                act.sem_inc(a_qk, FREE)
                act.sem_inc(a_v, FREE)
                act.sem_inc(a_kept, 2 * FREE)
                for e in range(2):
                    act.sem_inc(a_stored[e], 1)

                def step(b, u):
                    t = TPB * b + u
                    p = u % 2
                    if exists(t):
                        par, cols = u // HALF, slice(u % HALF * P, (u % HALF + 1) * P)
                        act.wait_ge(a_partt, FREE + t + 1)
                        if u % HALF == 0:
                            act.wait_ge(a_stored[par], 1 + 16 * nstores * b)
                        bank = ps[:, bank_pt + p, :].bitcast(BF16).rearrange("p (c n) -> p c n", n=P)
                        nc.scalar.copy(parts_t[:, par, 0:PC - 1, cols], bank[:, 0:PC - 1, :]).then_inc(a_kept, 1)
                        nc.scalar.copy(parts_t[0:PC_ROWS, par, PC - 1, cols],
                                       bank[0:PC_ROWS, PC - 1, :]).then_inc(a_kept, 1)
                    if exists(t + 4):
                        act.wait_ge(a_xt, FREE + t + 5)
                        act.wait_ge(a_proj, FREE + t + 3)
                        nc.scalar.copy(xhat_t[:, p].rearrange("p c n -> p (c n)"),
                                       ps[:, bank_xt + p, 0:D]).then_inc(a_xts, 1)
                    if exists(t + 3):
                        row, v = b + (u + 3) // TPB, (u + 3) % TPB
                        vpar, vu = v // HALF, v % HALF
                        act.wait_ge(a_proj, FREE + t + 4)
                        act.wait_ge(a_rope, 3 * FREE + 3 * (t + 2))
                        nc.scalar.copy(qk[:, 1 - p, :], ps[:, bank_qk + 1 - p, 0:QK]).then_inc(a_qk, 1)
                        if vu == 0:
                            act.wait_ge(a_stored[vpar], 1 + 16 * nstores * row)
                        nc.scalar.copy(v_out[:, vpar].rearrange("p g (n e) -> p g n e", e=DV)[:, :, vu, :],
                                       ps[:, bank_v + 1 - p, 0:D].rearrange("p (g e) -> p g e", e=DV)
                                       ).then_inc(a_v, 1)

                pipelined(act, step, 4)
                act.wait_ge(weights_in, 16 * nweights)

            @block.tensor
            def _(pe):
                pe.sem_inc(a_xt, FREE)
                pe.sem_inc(a_proj, FREE)
                pe.sem_inc(a_partt, FREE)
                pe.wait_ge(consts, 5)
                pe.wait_ge(a_scaled, 1)

                def step(b, u):
                    t = TPB * b + u
                    p = u % 2
                    if exists(t):
                        pe.wait_ge(a_split, t + 1)
                        pe.wait_ge(a_kept, 2 * FREE + 2 * (t - 1))
                        bank = ps[:, bank_pt + p, :].bitcast(BF16)
                        for c in range(PC):
                            n = min(P, PARTS * QK - c * P)
                            mm = nc.tensor.transpose(bank[0:n, c * P:(c + 1) * P],
                                                     parts[:, p, c * P:c * P + n], id16[:, :])
                        mm.then_inc(a_partt, 1)
                    if exists(t + 4):
                        pe.wait_ge(a_xhat, t + 5)
                        pe.wait_ge(a_xts, FREE + t + 3)
                        for c in range(DC):
                            mm = nc.tensor.transpose(ps[:, bank_xt + p, c * P:(c + 1) * P],
                                                     xhat[:, p, c * P:(c + 1) * P], id32[:, :])
                        mm.then_inc(a_xt, 1)
                    if exists(t + 3):
                        pe.wait_ge(a_xts, FREE + t + 4)
                        pe.wait_ge(a_qk, FREE + t + 2)
                        pe.wait_ge(a_v, FREE + t + 2)
                        for bank, lo, hi in ((bank_qk, 0, QK), (bank_v, QK, QKV)):
                            for c in range(DC):
                                mm = nc.tensor.matmul(ps[:, bank + 1 - p, 0:hi - lo], xhat_t[:, 1 - p, c, :],
                                                      wa[:, c, lo:hi], start=(c == 0), stop=(c == DC - 1))
                        mm.then_inc(a_proj, 1)

                pipelined(pe, step, 4)

        b_s1 = sem("b_s1")
        b_max = sem("b_max")
        b_exp1 = sem("b_exp1")
        b_ln = sem("b_ln")
        b_chain = sem("b_chain")
        b_parts = sem("b_parts")
        b_misc = sem("b_misc")
        b_read = sem("b_read")
        b_rows = sem("b_rows")
        b_shift = sem("b_shift")
        b_s2 = sem("b_s2")
        b_exp2 = sem("b_exp2")
        b_pv = sem("b_pv")
        b_ctx = sem("b_ctx")
        bank_s1, bank_s2, bank_ctx, bank_misc = 0, 4, 6, 7
        nchain = 4

        with nc.Block() as block:
            def body(eng, step):
                for s in range(STEPS):
                    step(0, 0, s)
                with rounds(nc, eng, GROUPS - 1, 2, start=1) as i1:
                    for e in (1, 0):
                        for s in range(STEPS):
                            step(i1 + (1 - e), e, s)
                for s in range(STEPS):
                    step(GROUPS - 1, 1, s)

            def projected(step, i, e, s):
                blk, into = s // TPB - 1, s % TPB
                for half, k, at in ((0, 0, 0), (0, 1, 2), (1, 0, 5), (1, 1, 7)):
                    if into == at:
                        nth = (0, 2, 5, 7)[blk + 1] + half * (2 if blk in (0, 2) else 1)
                        use = NMISC * i - 1 + nth
                        if blk < 0:
                            i, e, blk = i - 1, 1 - e, blk + 4
                        step(i, e, blk, half, k, use)

            def last(i):
                return isinstance(i, int) and i == GROUPS - 1

            def tile_at(i, e, n):
                if last(i) and n >= STEPS:
                    return None
                return (e + n // STEPS) % 2, n % STEPS // TPB, n % TPB

            @block.sync
            def _(sp):
                def put_shift(i, e, pair):
                    sp.wait_ge(b_rows, 2 * i + pair + 1)
                    sp.sem_inc(apart, 1)
                    for h in range(2):
                        sp.dma_start(q3[e][KS:KS + NSH, 2 * pair + h, :],
                                     shift_rows[pair][h * NSH:(h + 1) * NSH, :]).then_inc(b_shift, 16)

                def group(i, e, first=False):
                    if not first and not last(i):
                        sp.wait_ge(b_misc, NMISC * i + 1)
                        sp.sem_inc(apart, 1)
                    if not last(i):
                        fetch_wo(sp, i + 1, 1 - e)
                    put_shift(i, e, 1)
                    if not last(i):
                        put_shift(i + 1, 1 - e, 0)
                    if not isinstance(i, int) or i + 2 < GROUPS:
                        sp.wait_ge(b_pv, RING + STEPS * (i + 1))
                        sp.sem_inc(apart, 1)
                        fetch(sp, i + 2, e)

                for par in range(2):
                    sp.wait_ge(a_stored[par], 1 + 16 * nstores * B)
                put_shift(0, 0, 0)
                group(0, 0, first=True)
                with rounds(nc, sp, GROUPS - 3, 2, start=1) as i1:
                    for e in (1, 0):
                        group(i1 + (1 - e), e)
                for i in range(GROUPS - 3, GROUPS):
                    group(i, i % 2)

            @block.tensor
            def _(pe):
                pe.sem_inc(b_pv, RING)

                def scores_max(j, e, h, qt):
                    pair_bank = bank_s1 + 2 * (qt % 2)
                    pe.wait_ge(b_exp1, FREE + j - 1)
                    for k in range(2):
                        mm = nc.tensor.matmul(ps[:, pair_bank + k, :], q3[e][0:KS, h, qt * P:(qt + 1) * P],
                                              k3[e][0:KS, k * HT:(k + 1) * HT], start=True, stop=True)
                    mm.then_inc(b_s1, 1)

                def shift_rows_t(unit, use, pair):
                    pe.wait_ge(b_parts, unit + 1)
                    pe.wait_ge(b_read, use)
                    rows = ps[0:2 * NSH, bank_misc, :].bitcast(BF16)
                    for qt in range(TPB):
                        mm = nc.tensor.transpose(rows[:, qt * P:(qt + 1) * P],
                                                 shift_parts[:, qt].rearrange("p h k -> p (h k)"), id16[:, :])
                    mm.then_inc(b_misc, 1)

                def scores(i, e, s):
                    pair, qh, kt = s // 16, s // TPB % 2, s % TPB
                    pe.wait_ge(b_exp2, STEPS * i + s)
                    if s % 16 == 0:
                        pe.wait_ge(b_shift, 32 * (2 * i + pair + 1))
                    for h in range(2):
                        mm = nc.tensor.matmul(ps[:, bank_s2 + h, :], k3[e][0:KS + NSH, kt * P:(kt + 1) * P],
                                              q3[e][0:KS + NSH, 2 * pair + h, qh * HT:(qh + 1) * HT],
                                              start=True, stop=True)
                    mm.then_inc(b_s2, 1)

                def context(i, e, s):
                    kt = s % TPB
                    pe.wait_ge(b_exp2, STEPS * i + s + 1)
                    if kt == 0:
                        pe.wait_ge(b_ctx, 1 + 4 * i + s // TPB)
                    for h in range(2):
                        mm = nc.tensor.matmul(ps[h * DV:(h + 1) * DV, bank_ctx, :], vg[e][:, kt, :],
                                              probs[:, s % RING, h, :], start=(kt == 0), stop=(kt == TPB - 1))
                    mm.then_inc(b_pv, 1)

                def project(i, e, blk, half, k, use):
                    if k == 0:
                        pe.wait_ge(b_read, use)
                    if (half, k) == (0, 0):
                        pe.wait_ge(b_ctx, 1 + 4 * i + blk + 1)
                        if blk == 0:
                            pe.wait_ge(wo_loaded[e], 16 * (i // 2 + 1))
                    pair, qt = blk // 2, blk % 2 * HALF + 2 * half + k
                    mm = nc.tensor.matmul(ps[:, bank_misc, k * D:(k + 1) * D],
                                          ctx_t[:, pair, qt * P:(qt + 1) * P],
                                          wo[e][:, pair, :], start=True, stop=True)
                    if k == 1:
                        mm.then_inc(b_misc, 1)

                def step(i, e, s):
                    ahead = tile_at(i, e, s + LEAD)
                    if ahead is not None:
                        if s == STEPS - LEAD:
                            pe.wait_ge(b_loaded[1 - e], 16 * NFETCH * ((i + 1) // 2 + 1))
                        scores_max(STEPS * i + s + LEAD, *ahead)
                    if s < STEPS - 1:
                        scores(i, e, s + 1)
                    elif not last(i):
                        scores(i + 1, 1 - e, 0)
                    context(i, e, s)
                    if s == 12:
                        shift_rows_t(2 * i + 1, NMISC * i - 1 + 3, 1)
                    if s == 28 and not last(i):
                        shift_rows_t(2 * i + 2, NMISC * i - 1 + 8, 0)
                    if s >= TPB or not (isinstance(i, int) and i == 0):
                        gone = 1 if last(i) and s > 28 else 0
                        projected(lambda *a: project(*a[:-1], a[-1] - gone), i, e, s)

                pe.wait_ge(b_loaded[0], 16 * NFETCH)
                for j in range(LEAD):
                    scores_max(j, 0, j // TPB, j % TPB)
                    if j == 20:
                        shift_rows_t(0, 0, 0)
                scores(0, 0, 0)
                body(pe, step)
                for s in range(TPB):
                    projected(lambda *a: project(*a[:-1], a[-1] - 1), GROUPS, 0, s)

            @block.scalar
            def _(act):
                act.sem_inc(b_exp1, FREE)

                def sum_exp(j, e, h, qt):
                    pair_bank = bank_s1 + 2 * (qt % 2)
                    tile = ps[:, pair_bank:pair_bank + 2, :]
                    pair, col = h // 2, h % 2 * TPB + qt
                    act.wait_ge(b_max, j + 1)
                    nc.scalar.activation(tile, tile, ACT.Exp, bias=negm[:, pair, col:col + 1],
                                         accum_out=den[:, pair, col:col + 1]).then_inc(b_exp1, 1)

                def log_sum(unit, pair, j):
                    act.wait_ge(b_exp1, FREE + j + 1)
                    nc.scalar.activation(lnden[:, pair, :], den[:, pair, :], ACT.Ln).then_inc(b_ln, 1)

                def probabilities(i, s):
                    n = STEPS * i + s
                    act.wait_ge(b_s2, n + 1)
                    act.wait_ge(b_pv, n + 1)
                    nc.scalar.activation(probs[:, s % RING, :, :], ps[:, bank_s2:bank_s2 + 2, :],
                                         ACT.Exp).then_inc(b_exp2, 1)

                def step(i, e, s):
                    probabilities(i, s)
                    ahead = tile_at(i, e, s + LEAD - 1)
                    if ahead is not None:
                        sum_exp(STEPS * i + s + LEAD - 1, *ahead)
                    if s == 9:
                        log_sum(2 * i + 1, 1, STEPS * i + 31)
                    if s == 25 and not last(i):
                        log_sum(2 * i + 2, 0, STEPS * i + 47)

                for j in range(LEAD - 1):
                    sum_exp(j, 0, j // TPB, j % TPB)
                    if j == 16:
                        log_sum(0, 0, 15)
                body(act, step)

            @block.vector
            def _(dve):
                dve.sem_inc(b_ctx, 1)

                def row_max(j, e, h, qt):
                    pair_bank = bank_s1 + 2 * (qt % 2)
                    pair, col = h // 2, h % 2 * TPB + qt
                    dve.wait_ge(b_s1, j + 1)
                    nc.vector.tensor_reduce(negm[:, pair, col:col + 1], ps[:, pair_bank:pair_bank + 2, :],
                                            AX.XY, ALU.max, negate=True).then_inc(b_max, 1)

                def split_shift(unit, pair):
                    done = nchain * unit
                    out_part = [shift_parts[:, :, :, k].rearrange("p t h -> p h t") for k in range(NSH)]
                    by_head = [a[:, :].rearrange("p (h t) -> p h t", h=2) for a in (shift, shift_rest)]
                    dve.wait_ge(b_ln, unit + 1)
                    nc.vector.tensor_tensor(shift[:, :], negm[:, pair, :], lnden[:, pair, :],
                                            ALU.subtract).then_inc(b_chain, 1)
                    dve.wait_ge(b_chain, done + 1)
                    nc.vector.tensor_copy(out_part[0], by_head[0]).then_inc(b_chain, 1)
                    dve.wait_ge(b_chain, done + 2)
                    nc.vector.tensor_tensor(by_head[1], by_head[0], out_part[0], ALU.subtract).then_inc(b_chain, 1)
                    dve.wait_ge(b_chain, done + 3)
                    nc.vector.tensor_copy(out_part[1], by_head[1]).then_inc(b_chain, 1)
                    dve.wait_ge(b_chain, done + 4)
                    nc.vector.tensor_tensor(out_part[2], by_head[1], out_part[1], ALU.subtract).then_inc(b_parts, 1)

                def copy_rows(unit, use, pair):
                    dve.wait_ge(b_misc, use + 1)
                    nc.vector.tensor_copy(shift_rows[pair][:, :],
                                          ps[0:2 * NSH, bank_misc, :].bitcast(BF16)).then_inc(b_read, 1)
                    dve.wait_ge(b_read, use + 1)
                    dve.sem_inc(b_rows, 1)

                def keep_context(i, s):
                    pair, qh = s // 16, s // TPB % 2
                    dve.wait_ge(b_pv, RING + STEPS * i + s + 1)
                    nc.vector.tensor_copy(ctx_t[:, pair, qh * HT:(qh + 1) * HT],
                                          ps[:, bank_ctx, :]).then_inc(b_ctx, 1)

                def add_output(i, e, blk, half, k, use):
                    if k == 0:
                        return
                    dve.wait_ge(b_misc, use + 1)
                    rows = xs[:, bass.ds(i // KV * TPB + blk % 2 * HALF + 2 * half, 2), :]
                    nc.vector.tensor_tensor(rows, rows, ps[:, bank_misc, :].rearrange("p (k d) -> p k d", k=2),
                                            ALU.add).then_inc(b_read, 1)

                def step(i, e, s):
                    ahead = tile_at(i, e, s + LEAD)
                    if ahead is not None:
                        row_max(STEPS * i + s + LEAD, *ahead)
                    if s == 10:
                        split_shift(2 * i + 1, 1)
                    if s == 26 and not last(i):
                        split_shift(2 * i + 2, 0)
                    if s == 12:
                        copy_rows(2 * i + 1, NMISC * i - 1 + 3, 1)
                    if s == 28 and not last(i):
                        copy_rows(2 * i + 2, NMISC * i - 1 + 8, 0)
                    if s >= TPB or not (isinstance(i, int) and i == 0):
                        gone = 1 if last(i) and s > 28 else 0
                        projected(lambda *a: add_output(*a[:-1], a[-1] - gone), i, e, s)
                    if s % TPB == TPB - 1:
                        keep_context(i, s)

                for j in range(LEAD):
                    row_max(j, 0, j // TPB, j % TPB)
                    if j == 18:
                        split_shift(0, 0)
                    if j == 20:
                        copy_rows(0, 0, 0)
                body(dve, step)
                for s in range(TPB):
                    projected(lambda *a: add_output(*a[:-1], a[-1] - 1), GROUPS, 0, s)

        c_norm = sem("c_norm")
        c_var = sem("c_var")
        c_rstd = sem("c_rstd")
        c_xhat = sem("c_xhat")
        c_xt = sem("c_xt")
        c_xts = sem("c_xts")
        c_ff = sem("c_ff")
        c_gate = sem("c_gate")
        c_shifted = sem("c_shifted")
        c_exp = sem("c_exp")
        c_wexp = sem("c_wexp")
        c_hw = sem("c_hw")
        c_ht = sem("c_ht")
        c_hts = sem("c_hts")
        c_out = sem("c_out")
        c_y = sem("c_y")
        c_stored = [sem(f"c_stored{q}") for q in range(2)]
        bank_ff, bank_cxt, bank_ht = 0, 4, 6
        ngate = 10

        with nc.Block() as block:
            def idle(k, q):
                pass

            def sets(eng, first, front, back):
                first(0, 0)
                front(0, 0)
                first(1, 1)
                with rounds(nc, eng, SETS - 2, 2) as k2:
                    for q in range(2):
                        front(k2 + q + 1, 1 - q)
                        first(k2 + q + 2, q)
                        back(k2 + q, q)
                front(SETS - 1, 1)
                back(SETS - 2, 0)
                back(SETS - 1, 1)

            @block.sync
            def _(sp):
                for q in range(2):
                    sp.sem_inc(c_stored[q], 1)
                with rounds(nc, sp, SETS, 2) as k2:
                    for q in range(2):
                        k = k2 + q
                        sp.wait_ge(c_y, FREE + k + 1)
                        sp.sem_inc(apart, 1)
                        sp.dma_start(out_t[:, bass.ts(k, FSET), :], y[:, q]).then_inc(c_stored[q], 16)
                for q in range(2):
                    sp.wait_ge(c_stored[q], 1 + 16 * SETS // 2)

            @block.gpsimd
            def _(pool):
                def inverse_root(k, q):
                    slots = slice(FSET * q, FSET * (q + 1))
                    pool.wait_ge(c_var, k + 1)
                    nc.gpsimd.tensor_tensor(rstd[:, slots], var_eps[:, slots], neg_half[:, :],
                                            ALU.pow).then_inc(c_rstd, 1)

                sets(pool, inverse_root, idle, idle)

            @block.vector
            def _(dve):
                dve.sem_inc(c_y, FREE)

                def statistics(k, q):
                    slots = slice(FSET * q, FSET * (q + 1))
                    for u in range(FSET):
                        nc.vector.bn_stats(stats[:, FSET * q + u, :], xs[:, FSET * k + u, :]).then_inc(c_norm, 1)
                    for u in range(FSET):
                        dve.wait_ge(c_norm, 2 * FSET * k + FSET + u)
                        dve.sem_inc(apart, 1)
                        nc.vector.bn_aggr(moments[:, FSET * q + u, :],
                                          stats[:, FSET * q + u, :]).then_inc(c_norm, 1)
                    dve.wait_ge(c_norm, 2 * FSET * (k + 1))
                    nc.vector.tensor_scalar(var_eps[:, slots], moments[:, slots, 1], EPS, None,
                                            ALU.add).then_inc(c_var, 1)

                def front(k, q):
                    dve.wait_ge(c_rstd, k + 1)
                    for u in range(FSET):
                        t, slot = FSET * k + u, FSET * q + u
                        dve.wait_ge(c_xt, FREE + t - 1)
                        nc.vector.tensor_scalar(xhat[:, u, :], xs[:, t, :], moments[:, slot, 0:1],
                                                rstd[:, slot:slot + 1], ALU.subtract,
                                                ALU.mult).then_inc(c_xhat, 1)

                def back(k, q):
                    ff = ps[:, bank_ff + FSET * q:bank_ff + FSET * (q + 1), :]
                    h_shared, h_routed = ff[:, :, D:D + R], ff[:, :, D + R:D + NLR]
                    wide = [P, FSET, E]
                    done = ngate * k
                    dve.wait_ge(c_ff, FREE + FSET * (k + 1))
                    nc.vector.tensor_tensor(lg[:, q], ff[:, :, D + NLR:NF],
                                            br_row[:, :].unsqueeze(1).to_broadcast(wide), ALU.add).then_inc(c_gate, 1)
                    dve.wait_ge(c_gate, done + 1)
                    nc.vector.tensor_reduce(lmax[:, q], lg[:, q], AX.X, ALU.max).then_inc(c_gate, 1)
                    dve.wait_ge(c_gate, done + 2)
                    nc.vector.tensor_tensor(lexp[:, q], lg[:, q], lmax[:, q].unsqueeze(2).to_broadcast(wide),
                                            ALU.subtract).then_inc(c_shifted, 1)
                    dve.wait_ge(c_exp, k + 1)
                    nc.vector.tensor_reduce(lsum[:, q], lexp[:, q], AX.X, ALU.add).then_inc(c_gate, 1)
                    dve.wait_ge(c_gate, done + 3)
                    nc.vector.reciprocal(linv[:, q], lsum[:, q]).then_inc(c_gate, 1)
                    dve.wait_ge(c_gate, done + 4)
                    nc.vector.tensor_tensor(gates[:, q], lexp[:, q],
                                            linv[:, q].unsqueeze(2).to_broadcast(wide), ALU.mult).then_inc(c_gate, 1)
                    dve.wait_ge(c_gate, done + 5)
                    own = gates[:, q].rearrange("p f e -> p (f e)").unsqueeze(2).to_broadcast([P, FSET * E, E])
                    for f in range(FSET):
                        rows = slice(f * E, (f + 1) * E)
                        other = gates[:, q, f:f + 1, :].to_broadcast([P, E, E])
                        nc.vector.tensor_tensor(cge[:, q, rows, :], other, own[:, rows, :], ALU.is_ge)
                        last_cmp = nc.vector.tensor_tensor(cgt[:, q, rows, :], other, own[:, rows, :], ALU.is_gt)
                    last_cmp.then_inc(c_gate, 1)
                    dve.wait_ge(c_gate, done + 6)
                    nc.vector.tensor_tensor(cge[:, q], cge[:, q], cgt[:, q], ALU.subtract).then_inc(c_gate, 1)
                    dve.wait_ge(c_gate, done + 7)
                    tie = before_sb[:, :].rearrange("p (e j) -> p e j", j=E)
                    for f in range(FSET):
                        rows = slice(f * E, (f + 1) * E)
                        last_cmp = nc.vector.tensor_tensor(cge[:, q, rows, :], cge[:, q, rows, :], tie, ALU.mult)
                    last_cmp.then_inc(c_gate, 1)
                    dve.wait_ge(c_gate, done + 8)
                    nc.vector.tensor_tensor(cgt[:, q], cgt[:, q], cge[:, q], ALU.add).then_inc(c_gate, 1)
                    dve.wait_ge(c_gate, done + 9)
                    nc.vector.tensor_reduce(rank[:, q].rearrange("p f e -> p (f e)"), cgt[:, q], AX.X, ALU.add).then_inc(c_gate, 1)
                    dve.wait_ge(c_gate, done + 10)
                    nc.vector.scalar_tensor_tensor(out=wexp[:, q], in0=rank[:, q], scalar=float(TOP_K),
                                                   in1=gates[:, q], op0=ALU.is_lt,
                                                   op1=ALU.mult).then_inc(c_wexp, 1)
                    dve.wait_ge(c_ht, FREE + k - 1)
                    nc.vector.tensor_copy(hw[:, q, :, 0:R], h_shared).then_inc(c_hw, 1)
                    dve.wait_ge(c_wexp, k + 1)
                    for f in range(FSET):
                        last_hw = nc.vector.tensor_tensor(
                            hw[:, q, f, R:NLR].rearrange("p (e r) -> p e r", r=R),
                            h_routed[:, f, :].rearrange("p (e r) -> p e r", r=R),
                            wexp[:, q, f, :].unsqueeze(2).to_broadcast([P, E, R]), ALU.mult)
                        last_hw.then_inc(c_hw, 1)
                    dve.wait_ge(c_out, FREE + k + 1)
                    dve.wait_ge(c_stored[q], 1 + 16 * (k // 2))
                    nc.vector.tensor_tensor(y[:, q], xs[:, bass.ts(k, FSET), :], ff[:, :, 0:D],
                                            ALU.add).then_inc(c_y, 1)

                sets(dve, statistics, front, back)

            @block.scalar
            def _(act):
                act.sem_inc(c_xts, FREE)
                act.sem_inc(c_hts, FREE)

                def front(k, q):
                    for u in range(FSET):
                        t = FSET * k + u
                        act.wait_ge(c_xt, FREE + t + 1)
                        act.wait_ge(c_ff, FREE + t - 1)
                        nc.scalar.copy(xhat_t[:, u].rearrange("p c n -> p (c n)"),
                                       ps[:, bank_cxt + u, 0:D]).then_inc(c_xts, 1)

                def back(k, q):
                    act.wait_ge(c_shifted, k + 1)
                    nc.scalar.activation(lexp[:, q], lexp[:, q], ACT.Exp).then_inc(c_exp, 1)
                    act.wait_ge(c_ht, FREE + k + 1)
                    act.wait_ge(c_out, FREE + k - 1)
                    nc.scalar.copy(hw_t[:, q].rearrange("p f n -> p (f n)"),
                                   ps[0:NLR + 1, bank_ht + q, 0:FSET * P]).then_inc(c_hts, 1)

                sets(act, idle, front, back)

            @block.tensor
            def _(pe):
                pe.sem_inc(c_xt, FREE)
                pe.sem_inc(c_ff, FREE)
                pe.sem_inc(c_ht, FREE)
                pe.sem_inc(c_out, FREE)

                def front(k, q):
                    pe.wait_ge(c_y, FREE + k - 1)
                    for u in range(FSET):
                        t = FSET * k + u
                        pe.wait_ge(c_xhat, t + 1)
                        pe.wait_ge(c_xts, FREE + t - 1)
                        for c in range(DC):
                            mm = nc.tensor.transpose(ps[:, bank_cxt + u, c * P:(c + 1) * P],
                                                     xhat[:, u, c * P:(c + 1) * P], id32[:, :])
                        mm.then_inc(c_xt, 1)
                    for u in range(FSET):
                        t = FSET * k + u
                        pe.wait_ge(c_xts, FREE + t + 1)
                        for c in range(DC):
                            mm = nc.tensor.matmul(ps[:, bank_ff + FSET * q + u, 0:NF], xhat_t[:, u, c, :],
                                                  wf[:, c, :], start=(c == 0), stop=(c == DC - 1))
                        mm.then_inc(c_ff, 1)

                def back(k, q):
                    pe.wait_ge(c_hw, (FSET + 1) * (k + 1))
                    pe.wait_ge(c_hts, FREE + k - 1)
                    for f in range(FSET):
                        mm = nc.tensor.transpose(ps[0:NLR + 1, bank_ht + q, f * P:(f + 1) * P],
                                                 hw[:, q, f, :], id32[:, :])
                    mm.then_inc(c_ht, 1)
                    pe.wait_ge(c_hts, FREE + k + 1)
                    for f in range(FSET):
                        mm = nc.tensor.matmul(ps[:, bank_ff + FSET * q + f, 0:D], hw_t[:, q, f, :],
                                              wlr[:, :], start=False, stop=True, skip_group_check=True)
                    mm.then_inc(c_out, 1)

                sets(pe, idle, front, back)


_INS = ['L0_attn_x', 'L0_attn_W_attn', 'L0_attn_W_out', 'L0_attn_b_out', 'L0_ffn_W_base', 'L0_ffn_b_base',
        'L0_ffn_A_s', 'L0_ffn_B_s', 'L0_ffn_A_r', 'L0_ffn_B_r', 'L0_ffn_W_router', 'L0_ffn_b_router']


def kernel(**inputs):
    import numpy as _np
    import concourse.bacc as _bacc
    from concourse import mybir as _mybir
    from concourse.bass_utils import run_bass_kernel_spmd as _run

    f32 = _np.float32
    inv_freq = (f32(1.0) / _np.power(f32(10000.0), _np.arange(0, DK, 2, dtype=f32) / f32(DK))).astype(f32)
    ang = _np.arange(L, dtype=f32)[:, None] * inv_freq[None, :]
    cos, sin = _np.cos(ang), _np.sin(ang)
    table = _np.stack([_np.concatenate([cos, cos], 1), _np.concatenate([-sin, sin], 1)], 1)
    table = _np.ascontiguousarray(table.reshape(TPB, P, 2, DK).transpose(1, 0, 2, 3)).astype(f32)
    before = _np.broadcast_to(_np.tril(_np.ones((E, E), f32), -1).reshape(1, E * E), (P, E * E))
    consts = {"rope": table, "ident": _np.eye(P, dtype=f32), "before": _np.ascontiguousarray(before)}

    nc = _bacc.Bacc("TRN2", target_bir_lowering=False, num_devices=1)
    arrays, args = {}, []
    for name, a in [(n, _np.ascontiguousarray(inputs[n])) for n in _INS] + list(consts.items()):
        arrays[f"in_{name}_dram"] = a
        args.append(nc.dram_tensor(f"in_{name}_dram", a.shape, _mybir.dt.from_np(a.dtype), kind="ExternalInput").ap())
    args.append(nc.dram_tensor("out_0_dram", (B, L, D), F32, kind="ExternalOutput").ap())
    layer_kernel(nc, *args)
    r = _run(nc, [arrays], core_ids=[0])
    return r.results[0]["out_0_dram"]
```

```python
from contextlib import ExitStack, contextmanager

import concourse.bass as bass
from concourse import mybir

F32 = mybir.dt.float32
BF16 = mybir.dt.bfloat16
ALU = mybir.AluOpType
ACT = mybir.ActivationFunctionType
AX = mybir.AxisListType

P = 128
B, L, D = 4, 1024, 256
HEADS, KV = 16, 4
HPG = HEADS // KV
DK, DV = D // HEADS, D // KV
QK = HEADS * DK + KV * DK
QKV = QK + KV * DV
DC = D // P
TILES = B * L // P
TPB = L // P
HALF = TPB // 2
HT = HALF * P
GROUPS = B * KV
EPS = 1e-5
SCALE = DK ** -0.5

RUNS = ((0, 3, 0, 0), (3, 2, 1, 0), (5, 1, 2, 0))
SLOTS = 6
PARTS = 3
PC = -(-PARTS * QK // P)
PC_ROWS = PARTS * QK - (PC - 1) * P
KS = SLOTS * DK
NSH = 3

E, R, TOP_K = 6, 16, 2
NLR = R + E * R
NF = D + NLR + E
STEPS = 2 * 2 * TPB
LEAD = 24
RING = 8
NFETCH = 2 * len(RUNS) + 1
NMISC = 10
FSET = 2
SETS = TILES // FSET
FREE = 2


@contextmanager
def rounds(nc, eng, end, step, start=0):
    with eng.Fori(start, end, step) as i:
        yield nc.s_assert_within(i, start, end - step,
                                 skip_runtime_bounds_check_because="step divides end")


def layer_kernel(nc, x, w_attn, w_out, b_out, w_base, b_base, a_s, b_s, a_r, b_r,
                 w_router, b_router, rope, ident, masks, out):
    x_t = x.rearrange("b (t p) d -> p (b t) d", p=P)
    out_t = out.rearrange("b (t p) d -> p (b t) d", p=P)

    with ExitStack() as ctx:
        def sb(name, shape, dt=F32):
            return ctx.enter_context(nc.sbuf_tensor(name, shape, dt))

        def sem(name):
            return ctx.enter_context(nc.semaphore(name))

        qk_dram = nc.dram_tensor("qk_parts", [B, PARTS * QK, L], BF16).ap()
        v_dram = nc.dram_tensor("v_rows", [B, KV, P, TPB * DV], F32).ap()

        xs = sb("xs", [P, TILES, D])
        wa = sb("wa", [P, DC, QKV])
        wf = sb("wf", [P, DC, NF])
        wlr = sb("wlr", [NLR + 1, D])
        bo_row = sb("bo_row", [P, D])
        br_row = sb("br_row", [P, E])
        rope_sb = sb("rope_sb", [P, TPB, 2, DK])
        id32 = sb("id32", [P, P])
        id16 = sb("id16", [P, P], BF16)
        masks_sb = sb("masks_sb", [P, E * 2 * E])

        stats = sb("stats", [P, 4, 6])
        moments = sb("moments", [P, 4, 2])
        var_eps = sb("var_eps", [P, 4])
        rstd = sb("rstd", [P, 4])
        neg_half = sb("neg_half", [P, 2])
        xhat = sb("xhat", [P, 4, D])
        xhat_t = sb("xhat_t", [P, 4, DC, P])

        qk = sb("qk", [P, 2, QK])
        rope_c = sb("rope_c", [P, 2, QK])
        rope_s = sb("rope_s", [P, 2, QK])
        qkr = sb("qkr", [P, QK])
        rest = sb("rest", [P, QK])
        parts = sb("parts", [P, 2, PARTS * QK], BF16)
        parts_t = sb("parts_t", [P, 2, PC, HT], BF16)
        v_out = sb("v_out", [P, 2, KV, HALF * DV])

        q3 = [sb(f"q3_{e}", [P, HPG, L], BF16) for e in range(2)]
        k3 = [sb(f"k3_{e}", [P, L], BF16) for e in range(2)]
        vg = [sb(f"vg_{e}", [P, TPB, DV]) for e in range(2)]
        wo = [sb(f"wo_{e}", [P, 2, D]) for e in range(2)]
        probs = sb("probs", [P, RING, 2, HT])
        negm = sb("negm", [P, 2, 2 * TPB])
        den = sb("den", [P, 2, 2 * TPB])
        lnden = sb("lnden", [P, 2, 2 * TPB])
        shift = sb("shift", [P, 2 * TPB])
        shift_rest = sb("shift_rest", [P, 2 * TPB])
        shift_parts = sb("shift_parts", [P, TPB, 2, NSH], BF16)
        shift_rows = [sb(f"shift_rows_{q}", [2 * NSH, L], BF16) for q in range(2)]
        ctx_t = sb("ctx_t", [P, 2, L])

        lg = sb("lg", [P, 2, FSET, E])
        lmax = sb("lmax", [P, 2, FSET])
        lexp = sb("lexp", [P, 2, FSET, E])
        lsum = sb("lsum", [P, 2, FSET])
        linv = sb("linv", [P, 2, FSET])
        gates = sb("gates", [P, 2, FSET, E])
        above = sb("above", [P, 2, FSET, E, 2, E])
        rank = sb("rank", [P, 2, FSET, E])
        wexp = sb("wexp", [P, 2, FSET, E])
        hw = sb("hw", [P, 2, FSET, NLR + 1])
        hw_t = sb("hw_t", [NLR + 1, 2, FSET, P])
        y = sb("y", [P, 2, FSET, D])

        apart = sem("apart")
        ps = ctx.enter_context(nc.psum_tensor("ps", [P, 8, 512], F32))

        first_in = sem("first_in")
        weights_in = sem("weights_in")
        x_in = [sem(f"x_in{e}") for e in range(2)]
        consts = sem("consts")
        a_scaled = sem("a_scaled")
        a_norm = sem("a_norm")
        a_var = sem("a_var")
        a_rstd = sem("a_rstd")
        a_xhat = sem("a_xhat")
        a_xt = sem("a_xt")
        a_xts = sem("a_xts")
        a_proj = sem("a_proj")
        a_qk = sem("a_qk")
        a_v = sem("a_v")
        a_rope = sem("a_rope")
        a_roped = sem("a_roped")
        a_part0 = sem("a_part0")
        a_rest = sem("a_rest")
        a_part1 = sem("a_part1")
        a_split = sem("a_split")
        a_partt = sem("a_partt")
        a_kept = sem("a_kept")
        a_stored = [sem(f"a_stored{e}") for e in range(2)]
        b_loaded = [sem(f"b_loaded{e}") for e in range(2)]
        wo_loaded = [sem(f"wo_loaded{e}") for e in range(2)]
        nfirst = 3
        nweights = 3 + 2 * DC + 5
        nstores = 3
        bank_xt, bank_qk, bank_v, bank_pt = 0, 2, 4, 6

        def pipelined(eng, step, lead):
            for u in range(-lead, 0):
                step(0, u)
            with rounds(nc, eng, B - 1, 1) as b:
                for u in range(TPB):
                    step(b, u)
            for u in range(TPB):
                step(B - 1, u)

        def exists(t):
            return not isinstance(t, int) or 0 <= t < TILES

        def store(sp, b, par):
            hb = 2 * b + par
            sp.wait_ge(a_v, FREE + HALF * (hb + 1))
            sp.sem_inc(apart, 1)
            vcols = slice(par * HALF * DV, (par + 1) * HALF * DV)
            sp.dma_start(v_dram[b, :, :, vcols].rearrange("g p n -> p g n"),
                         v_out[:, par, :, :]).then_inc(a_stored[par], 16)
            sp.wait_ge(a_kept, 2 * FREE + 2 * HALF * (hb + 1))
            sp.sem_inc(apart, 1)
            cols = slice(par * HT, (par + 1) * HT)
            full = (PC - 1) * P
            sp.dma_start(qk_dram[b, 0:full, cols].rearrange("(c p) t -> p c t", p=P),
                         parts_t[:, par, 0:PC - 1, :]).then_inc(a_stored[par], 16)
            sp.dma_start(qk_dram[b, full:PARTS * QK, cols],
                         parts_t[0:PC_ROWS, par, PC - 1, :]).then_inc(a_stored[par], 16)

        def fetch(sp, i, e):
            b, g = i // KV, i % KV
            done = b_loaded[e]
            by_part = qk_dram[b].rearrange("(k r) t -> k r t", k=PARTS)
            for slot, n, qp, kp in RUNS:
                rows = slice(slot * DK, (slot + n) * DK)
                q_rows = by_part[qp:qp + 1, bass.ts(g, DK * HPG), :].rearrange("k (d h) t -> k d (h t)", h=HPG)
                k_rows = by_part[kp:kp + n, HEADS * DK:QK, :].rearrange("k (d h) t -> k d h t", h=KV)[:, :, g, :]
                sp.dma_start(q3[e][rows, :, :].rearrange("r h t -> r (h t)"),
                             q_rows.to_broadcast([n, DK, HPG * L])).then_inc(done, 16)
                sp.dma_start(k3[e][rows, :], k_rows).then_inc(done, 16)
            sp.dma_start(vg[e][:, :, :].rearrange("p k e -> p (k e)"), v_dram[b, g, :, :]).then_inc(done, 16)

        def fetch_wo(sp, i, e):
            sp.dma_start(wo[e][:, :, :],
                         w_out[bass.ts(i % KV, HPG * DV), :].rearrange("(q p) n -> p q n", p=P)
                         ).then_inc(wo_loaded[e], 16)

        with nc.Block() as block:
            @block.sync
            def _(sp):
                def load(dst, src):
                    sp.dma_start(dst, src).then_inc(weights_in, 16)

                def load_x(hb, par):
                    sp.dma_start(xs[:, bass.ts(hb, HALF), :],
                                 x_t[:, bass.ts(hb, HALF), :]).then_inc(x_in[par], 16)

                def half_row(b, par, last=False):
                    if not last:
                        sp.wait_ge(x_in[par], 16 * (b + 1))
                        sp.sem_inc(apart, 1)
                        load_x(2 * b + par + 2, par)
                    store(sp, b, par)

                load_x(0, 0)
                sp.wait_ge(x_in[0], 16)
                load_x(1, 1)
                load(bo_row[:, :], b_out.partition_broadcast(P))
                load(br_row[:, :], b_router.partition_broadcast(P))
                load(masks_sb[:, :], masks)
                for c in range(DC):
                    rows = slice(c * P, (c + 1) * P)
                    load(wf[:, c, 0:D], w_base[rows, :])
                    load(wf[:, c, D + R:D + NLR].rearrange("p (e r) -> p e r", r=R),
                         a_r[:, rows, :].rearrange("e p r -> p e r"))
                load(wf[:, :, D:D + R], a_s.rearrange("(c p) r -> p c r", p=P))
                load(wf[:, :, D + NLR:NF], w_router.rearrange("(c p) e -> p c e", p=P))
                load(wlr[0:R, :], b_s)
                load(wlr[R:NLR, :], b_r.rearrange("e r d -> (e r) d"))
                load(wlr[NLR:NLR + 1, :], b_base.unsqueeze(0))
                with rounds(nc, sp, B - 1, 1) as b:
                    half_row(b, 0)
                    half_row(b, 1)
                for par in range(2):
                    sp.wait_ge(a_stored[par], 1 + 16 * nstores)
                for i in range(2):
                    fetch(sp, i, i)
                fetch_wo(sp, 0, 0)
                half_row(B - 1, 0, last=True)

            @block.gpsimd
            def _(pool):
                pool.sem_inc(a_rope, 3 * FREE)
                for e in range(2):
                    nc.gpsimd.memset(k3[e][KS:P, :], 1.0).then_inc(consts, 1)
                pool.wait_ge(consts, 4)
                nh, half = QK // DK, DK // 2

                def rotate(t, u):
                    p = u % 2
                    xv, cv, sv = (a[:, p, :].rearrange("p (h i) -> p h i", i=DK) for a in (qk, rope_c, rope_s))

                    def table(k, lo, hi):
                        return rope_sb[:, u:u + 1, k, lo:hi].to_broadcast([P, nh, hi - lo])

                    pool.wait_ge(a_qk, FREE + t + 1)
                    pool.wait_ge(a_roped, FREE + t - 1)
                    nc.gpsimd.tensor_tensor(cv, xv, table(0, 0, DK), ALU.mult).then_inc(a_rope, 1)
                    nc.gpsimd.tensor_tensor(sv[:, :, 0:half], xv[:, :, half:DK], table(1, 0, half),
                                            ALU.mult).then_inc(a_rope, 1)
                    nc.gpsimd.tensor_tensor(sv[:, :, half:DK], xv[:, :, 0:half], table(1, half, DK),
                                            ALU.mult).then_inc(a_rope, 1)

                def step(b, u):
                    t = TPB * b + u
                    if isinstance(b, int) and t == -2:
                        pool.wait_ge(first_in, 16 * nfirst)
                    if exists(t + 2):
                        rotate(t + 2, (u + 2) % TPB)
                    if exists(t + 6):
                        slot = slice((u + 6) % 4, (u + 6) % 4 + 1)
                        pool.wait_ge(a_var, t + 7)
                        nc.gpsimd.tensor_tensor(rstd[:, slot], var_eps[:, slot], neg_half[:, 0:1],
                                                ALU.pow).then_inc(a_rstd, 1)

                pipelined(pool, step, 6)

            @block.vector
            def _(dve):
                nc.vector.memset(hw[:, :, :, NLR:NLR + 1], 1.0).then_inc(consts, 1)
                nc.vector.memset(neg_half[:, :], -0.5).then_inc(consts, 1)
                dve.sem_inc(a_roped, FREE)

                def step(b, u):
                    t = TPB * b + u
                    split, norm, new = exists(t + 1), exists(t + 5), exists(t + 6)
                    p, slot, new_slot = (u + 1) % 2, (u + 5) % 4, (u + 6) % 4
                    part = [parts[:, p, k * QK:(k + 1) * QK] for k in range(PARTS)]
                    if isinstance(b, int) and t == -4:
                        dve.wait_ge(first_in, 16 * nfirst)
                        nc.vector.tensor_copy(id16[:, :], id32[:, :]).then_inc(a_scaled, 1)
                        nc.vector.tensor_scalar(wa[:, :, 0:HEADS * DK], wa[:, :, 0:HEADS * DK], SCALE, None,
                                                ALU.mult).then_inc(a_scaled, 1)
                    if split:
                        dve.wait_ge(a_rope, 3 * FREE + 3 * (t + 2))
                        by_dim = qkr[:, :].rearrange("p (b i h) -> p b h i", i=DK, h=HPG)
                        c, s = (a[:, p, :].rearrange("p (b h i) -> p b h i", i=DK, h=HPG) for a in (rope_c, rope_s))
                        nc.vector.tensor_tensor(by_dim, c, s, ALU.add).then_inc(a_roped, 1)
                    if norm:
                        dve.wait_ge(a_rstd, t + 6)
                        dve.wait_ge(a_xt, FREE + t + 4)
                        nc.vector.tensor_scalar(xhat[:, 1 - u % 2, :], xs[:, t + 5, :], moments[:, slot, 0:1],
                                                rstd[:, slot:slot + 1], ALU.subtract, ALU.mult).then_inc(a_xhat, 1)
                    if split:
                        dve.wait_ge(a_roped, FREE + t + 2)
                        dve.wait_ge(a_partt, FREE + t)
                        nc.vector.tensor_copy(part[0], qkr[:, :]).then_inc(a_part0, 1)
                    if new:
                        if (u + 6) % HALF == 0:
                            row, half = b + (u + 6) // TPB, (u + 6) % TPB // HALF
                            dve.wait_ge(x_in[half], 16 * (row + 1))
                        nc.vector.bn_stats(stats[:, new_slot, :], xs[:, t + 6, :]).then_inc(a_norm, 1)
                    if split:
                        dve.wait_ge(a_part0, t + 2)
                        nc.vector.tensor_tensor(rest[:, :], qkr[:, :], part[0], ALU.subtract).then_inc(a_rest, 1)
                    if new:
                        dve.wait_ge(a_norm, 2 * t + 13)
                        dve.sem_inc(apart, 1)
                        nc.vector.bn_aggr(moments[:, new_slot, :], stats[:, new_slot, :]).then_inc(a_norm, 1)
                    if split:
                        dve.wait_ge(a_rest, t + 2)
                        nc.vector.tensor_copy(part[1], rest[:, :]).then_inc(a_part1, 1)
                    if new:
                        dve.wait_ge(a_norm, 2 * t + 14)
                        nc.vector.tensor_scalar(var_eps[:, new_slot:new_slot + 1], moments[:, new_slot, 1:2], EPS,
                                                None, ALU.add).then_inc(a_var, 1)
                    if split:
                        dve.wait_ge(a_part1, t + 2)
                        nc.vector.tensor_tensor(part[2], rest[:, :], part[1], ALU.subtract).then_inc(a_split, 1)

                pipelined(dve, step, 6)

            @block.scalar
            def _(act):
                def load(dst, src):
                    act.dma_start(dst, src).then_inc(first_in, 16)

                load(wa[:, :, :], w_attn.rearrange("(c p) n -> p c n", p=P))
                load(id32[:, :], ident)
                load(rope_sb[:, :, :, :], rope)
                nc.scalar.preload_act_table_set("natural_log_exp_and_others")
                act.sem_inc(a_xts, FREE)
                act.sem_inc(a_qk, FREE)
                act.sem_inc(a_v, FREE)
                act.sem_inc(a_kept, 2 * FREE)
                for e in range(2):
                    act.sem_inc(a_stored[e], 1)

                def step(b, u):
                    t = TPB * b + u
                    p = u % 2
                    if exists(t):
                        par, cols = u // HALF, slice(u % HALF * P, (u % HALF + 1) * P)
                        act.wait_ge(a_partt, FREE + t + 1)
                        if u % HALF == 0:
                            act.wait_ge(a_stored[par], 1 + 16 * nstores * b)
                        bank = ps[:, bank_pt + p, :].bitcast(BF16).rearrange("p (c n) -> p c n", n=P)
                        nc.scalar.copy(parts_t[:, par, 0:PC - 1, cols], bank[:, 0:PC - 1, :]).then_inc(a_kept, 1)
                        nc.scalar.copy(parts_t[0:PC_ROWS, par, PC - 1, cols],
                                       bank[0:PC_ROWS, PC - 1, :]).then_inc(a_kept, 1)
                    if exists(t + 4):
                        act.wait_ge(a_xt, FREE + t + 5)
                        act.wait_ge(a_proj, FREE + t + 3)
                        nc.scalar.copy(xhat_t[:, p].rearrange("p c n -> p (c n)"),
                                       ps[:, bank_xt + p, 0:D]).then_inc(a_xts, 1)
                    if exists(t + 3):
                        row, v = b + (u + 3) // TPB, (u + 3) % TPB
                        vpar, vu = v // HALF, v % HALF
                        act.wait_ge(a_proj, FREE + t + 4)
                        act.wait_ge(a_rope, 3 * FREE + 3 * (t + 2))
                        nc.scalar.copy(qk[:, 1 - p, :], ps[:, bank_qk + 1 - p, 0:QK]).then_inc(a_qk, 1)
                        if vu == 0:
                            act.wait_ge(a_stored[vpar], 1 + 16 * nstores * row)
                        nc.scalar.copy(v_out[:, vpar].rearrange("p g (n e) -> p g n e", e=DV)[:, :, vu, :],
                                       ps[:, bank_v + 1 - p, 0:D].rearrange("p (g e) -> p g e", e=DV)
                                       ).then_inc(a_v, 1)

                pipelined(act, step, 4)
                act.wait_ge(weights_in, 16 * nweights)

            @block.tensor
            def _(pe):
                pe.sem_inc(a_xt, FREE)
                pe.sem_inc(a_proj, FREE)
                pe.sem_inc(a_partt, FREE)
                pe.wait_ge(a_scaled, 2)

                def step(b, u):
                    t = TPB * b + u
                    p = u % 2
                    if exists(t):
                        pe.wait_ge(a_split, t + 1)
                        pe.wait_ge(a_kept, 2 * FREE + 2 * (t - 1))
                        bank = ps[:, bank_pt + p, :].bitcast(BF16)
                        for c in range(PC):
                            n = min(P, PARTS * QK - c * P)
                            mm = nc.tensor.transpose(bank[0:n, c * P:(c + 1) * P],
                                                     parts[:, p, c * P:c * P + n], id16[:, :])
                        mm.then_inc(a_partt, 1)
                    if exists(t + 4):
                        pe.wait_ge(a_xhat, t + 5)
                        pe.wait_ge(a_xts, FREE + t + 3)
                        for c in range(DC):
                            mm = nc.tensor.transpose(ps[:, bank_xt + p, c * P:(c + 1) * P],
                                                     xhat[:, p, c * P:(c + 1) * P], id32[:, :])
                        mm.then_inc(a_xt, 1)
                    if exists(t + 3):
                        pe.wait_ge(a_xts, FREE + t + 4)
                        pe.wait_ge(a_qk, FREE + t + 2)
                        pe.wait_ge(a_v, FREE + t + 2)
                        for bank, lo, hi in ((bank_qk, 0, QK), (bank_v, QK, QKV)):
                            for c in range(DC):
                                mm = nc.tensor.matmul(ps[:, bank + 1 - p, 0:hi - lo], xhat_t[:, 1 - p, c, :],
                                                      wa[:, c, lo:hi], start=(c == 0), stop=(c == DC - 1))
                        mm.then_inc(a_proj, 1)

                pipelined(pe, step, 4)

        b_s1 = sem("b_s1")
        b_max = sem("b_max")
        b_exp1 = sem("b_exp1")
        b_ln = sem("b_ln")
        b_chain = sem("b_chain")
        b_parts = sem("b_parts")
        b_misc = sem("b_misc")
        b_read = sem("b_read")
        b_shift = sem("b_shift")
        b_bias = sem("b_bias")
        b_s2 = sem("b_s2")
        b_exp2 = sem("b_exp2")
        b_pv = sem("b_pv")
        b_ctx = sem("b_ctx")
        bank_s1, bank_s2, bank_ctx, bank_misc = 0, 4, 6, 7
        nchain = 4

        c_norm = sem("c_norm")
        c_var = sem("c_var")
        c_rstd = sem("c_rstd")
        c_xhat = sem("c_xhat")
        c_xt = sem("c_xt")
        c_xts = sem("c_xts")
        c_ff = sem("c_ff")
        c_gate = sem("c_gate")
        c_shifted = sem("c_shifted")
        c_exp = sem("c_exp")
        c_wexp = sem("c_wexp")
        c_hw = sem("c_hw")
        c_ht = sem("c_ht")
        c_hts = sem("c_hts")
        c_out = sem("c_out")
        c_y = sem("c_y")
        c_stored = [sem(f"c_stored{q}") for q in range(2)]
        bank_cxt, bank_ht, bank_ff = 0, 2, 4
        ngate = 9

        def real(k):
            return not isinstance(k, int) or 0 <= k < SETS

        def set_statistics(dve, k, q, u):
            slot = FSET * q + u
            nc.vector.bn_stats(stats[:, slot, :], xs[:, FSET * k + u, :]).then_inc(c_norm, 1)

        def set_aggregate(dve, k, q, u):
            slot = FSET * q + u
            dve.wait_ge(c_norm, 2 * FSET * k + FSET + u)
            dve.sem_inc(apart, 1)
            nc.vector.bn_aggr(moments[:, slot, :], stats[:, slot, :]).then_inc(c_norm, 1)

        def set_variance(dve, k, q):
            slots = slice(FSET * q, FSET * (q + 1))
            dve.wait_ge(c_norm, 2 * FSET * (k + 1))
            nc.vector.tensor_scalar(var_eps[:, slots], moments[:, slots, 1], EPS, None,
                                    ALU.add).then_inc(c_var, 1)

        def set_norm(dve, k, q, u):
            slot = FSET * q + u
            if u == 0:
                dve.wait_ge(c_rstd, k + 1)
                dve.wait_ge(c_xt, FREE + k - 1)
            nc.vector.tensor_scalar(xhat[:, slot, :], xs[:, FSET * k + u, :], moments[:, slot, 0:1],
                                    rstd[:, slot:slot + 1], ALU.subtract, ALU.mult).then_inc(c_xhat, 1)

        def set_rstd(pool, k, q):
            slots = slice(FSET * q, FSET * (q + 1))
            pool.wait_ge(c_var, k + 1)
            nc.gpsimd.tensor_tensor(rstd[:, slots], var_eps[:, slots], neg_half[:, :],
                                    ALU.pow).then_inc(c_rstd, 1)

        def set_copy(act, k, q):
            act.wait_ge(c_xt, FREE + k + 1)
            act.wait_ge(c_ff, FREE + k - 1)
            nc.scalar.copy(xhat_t[:, FSET * q:FSET * (q + 1)].rearrange("p f c n -> p (f c n)"),
                           ps[:, bank_cxt + q, :]).then_inc(c_xts, 1)

        def set_transpose(pe, k, q):
            pe.wait_ge(c_xhat, FSET * (k + 1))
            pe.wait_ge(c_xts, FREE + k - 1)
            for u in range(FSET):
                for c in range(DC):
                    mm = nc.tensor.transpose(ps[:, bank_cxt + q, (u * DC + c) * P:(u * DC + c + 1) * P],
                                             xhat[:, FSET * q + u, c * P:(c + 1) * P], id32[:, :])
            mm.then_inc(c_xt, 1)

        with nc.Block() as block:
            def body(eng, step):
                for s in range(STEPS):
                    step(0, 0, s)
                with rounds(nc, eng, GROUPS - 1, 2, start=1) as i1:
                    for e in (1, 0):
                        for s in range(STEPS):
                            step(i1 + (1 - e), e, s)
                for s in range(STEPS):
                    step(GROUPS - 1, 1, s)

            uses = ((-1, 0), (-1, 1), (0, 0), "shift", (0, 1), (1, 0), (1, 1), (2, 0), "next shift", (2, 1))

            def used(i, what):
                gone = isinstance(i, int) and (i >= GROUPS or i == GROUPS - 1 and what == (2, 1))
                return NMISC * i - 1 + uses.index(what) - (1 if gone else 0)

            def projected(step, i, e, s):
                blk = s // TPB - 1
                with_shift = {1: (0, 0), 2: (0, 1), 5: (1, 0), 7: (1, 1)}
                without = {1: (0, 0), 3: (0, 1), 5: (1, 0), 7: (1, 1)}
                tile = (with_shift if blk in (0, 2) else without).get(s % TPB)
                if tile is not None:
                    half, k = tile
                    if blk >= 0:
                        step(i, e, blk, half, k, used(i, (blk, half)))
                    elif not (isinstance(i, int) and i == 0):
                        step(i - 1, 1 - e, blk + 4, half, k, used(i, (blk, half)))

            def last(i):
                return isinstance(i, int) and i == GROUPS - 1

            def s1_bank(j, qt, slots):
                return bank_s1 + 2 * (j % slots if slots == 3 else qt % 2)

            def tile_at(i, e, n):
                if last(i) and n >= STEPS:
                    return None
                return (e + n // STEPS) % 2, n % STEPS // TPB, n % TPB

            @block.sync
            def _(sp):
                def put_shift(use, e, pair):
                    sp.wait_ge(b_read, use + 1)
                    sp.sem_inc(apart, 1)
                    for h in range(2):
                        sp.dma_start(q3[e][KS:KS + NSH, 2 * pair + h, :],
                                     shift_rows[pair][h * NSH:(h + 1) * NSH, :]).then_inc(b_shift, 16)

                def group(i, e, first=False):
                    if not first and not last(i):
                        sp.wait_ge(b_misc, NMISC * i + 1)
                        sp.sem_inc(apart, 1)
                    if not last(i):
                        fetch_wo(sp, i + 1, 1 - e)
                    put_shift(used(i, "shift"), e, 1)
                    if not last(i):
                        put_shift(used(i, "next shift"), 1 - e, 0)
                    if not isinstance(i, int) or i + 2 < GROUPS:
                        sp.wait_ge(b_pv, RING + STEPS * (i + 1))
                        sp.sem_inc(apart, 1)
                        fetch(sp, i + 2, e)

                store(sp, B - 1, 1)
                for par in range(2):
                    sp.wait_ge(a_stored[par], 1 + 16 * nstores * B)
                put_shift(0, 0, 0)
                group(0, 0, first=True)
                with rounds(nc, sp, GROUPS - 3, 2, start=1) as i1:
                    for e in (1, 0):
                        group(i1 + (1 - e), e)
                for i in range(GROUPS - 3, GROUPS):
                    group(i, i % 2)

            @block.gpsimd
            def _(pool):
                for k in range(4):
                    set_rstd(pool, k, k % 2)

            @block.tensor
            def _(pe):
                pe.sem_inc(b_pv, RING)
                for done in (c_xt, c_ff, c_ht):
                    pe.sem_inc(done, FREE)
                pe.sem_inc(c_out, FSET * FREE)

                def scores_max(j, e, h, qt, slots=2):
                    pair_bank = s1_bank(j, qt, slots)
                    if slots == 2 or j >= slots:
                        pe.wait_ge(b_exp1, FREE + j - slots + 1)
                    for k in range(2):
                        mm = nc.tensor.matmul(ps[:, pair_bank + k, :], q3[e][0:KS, h, qt * P:(qt + 1) * P],
                                              k3[e][0:KS, k * HT:(k + 1) * HT], start=True, stop=True)
                    mm.then_inc(b_s1, 1)

                def shift_rows_t(unit, use, pair):
                    pe.wait_ge(b_parts, unit + 1)
                    pe.wait_ge(b_read, use)
                    rows = ps[0:2 * NSH, bank_misc, :].bitcast(BF16)
                    for qt in range(TPB):
                        mm = nc.tensor.transpose(rows[:, qt * P:(qt + 1) * P],
                                                 shift_parts[:, qt].rearrange("p h k -> p (h k)"), id16[:, :])
                    mm.then_inc(b_misc, 1)

                def scores(i, e, s):
                    pair, qh, kt = s // 16, s // TPB % 2, s % TPB
                    pe.wait_ge(b_exp2, STEPS * i + s)
                    if s % 16 == 0:
                        pe.wait_ge(b_shift, 32 * (2 * i + pair + 1))
                    for h in range(2):
                        mm = nc.tensor.matmul(ps[:, bank_s2 + h, :], k3[e][0:KS + NSH, kt * P:(kt + 1) * P],
                                              q3[e][0:KS + NSH, 2 * pair + h, qh * HT:(qh + 1) * HT],
                                              start=True, stop=True)
                    mm.then_inc(b_s2, 1)

                def context(i, e, s):
                    kt = s % TPB
                    pe.wait_ge(b_exp2, STEPS * i + s + 1)
                    if kt == 0:
                        pe.wait_ge(b_ctx, 1 + 4 * i + s // TPB)
                    for h in range(2):
                        mm = nc.tensor.matmul(ps[h * DV:(h + 1) * DV, bank_ctx, :], vg[e][:, kt, :],
                                              probs[:, s % RING, h, :], start=(kt == 0), stop=(kt == TPB - 1))
                    mm.then_inc(b_pv, 1)

                def project(i, e, blk, half, k, use):
                    if k == 0:
                        pe.wait_ge(b_read, use)
                    if (half, k) == (0, 0):
                        pe.wait_ge(b_ctx, 1 + 4 * i + blk + 1)
                        if blk == 0:
                            pe.wait_ge(wo_loaded[e], 16 * (i // 2 + 1))
                    pair, qt = blk // 2, blk % 2 * HALF + 2 * half + k
                    mm = nc.tensor.matmul(ps[:, bank_misc, k * D:(k + 1) * D],
                                          ctx_t[:, pair, qt * P:(qt + 1) * P],
                                          wo[e][:, pair, :], start=True, stop=True)
                    if k == 1:
                        mm.then_inc(b_misc, 1)

                def step(i, e, s):
                    ahead = tile_at(i, e, s + LEAD)
                    if ahead is not None:
                        if s == STEPS - LEAD:
                            pe.wait_ge(b_loaded[1 - e], 16 * NFETCH * ((i + 1) // 2 + 1))
                        scores_max(STEPS * i + s + LEAD, *ahead)
                    if s < STEPS - 1:
                        scores(i, e, s + 1)
                    elif not last(i):
                        scores(i + 1, 1 - e, 0)
                    context(i, e, s)
                    if s == 12:
                        shift_rows_t(2 * i + 1, used(i, "shift"), 1)
                    if s == 28 and not last(i):
                        shift_rows_t(2 * i + 2, used(i, "next shift"), 0)
                    projected(project, i, e, s)
                    if last(i) and s in (18, 22):
                        k = (s - 18) // 4
                        set_transpose(pe, k, k)

                pe.wait_ge(b_loaded[0], 16 * NFETCH)
                for j in range(LEAD):
                    scores_max(j, 0, j // TPB, j % TPB, slots=3 if j < LEAD - 3 else 2)
                    if j == 20:
                        shift_rows_t(0, 0, 0)
                scores(0, 0, 0)
                body(pe, step)
                for s in range(TPB):
                    projected(project, GROUPS, 0, s)

            @block.scalar
            def _(act):
                act.sem_inc(b_exp1, FREE)
                for done in (c_xts, c_hts):
                    act.sem_inc(done, FREE)

                def sum_exp(j, e, h, qt, slots=2):
                    pair_bank = s1_bank(j, qt, slots)
                    tile = ps[:, pair_bank:pair_bank + 2, :]
                    pair, col = h // 2, h % 2 * TPB + qt
                    act.wait_ge(b_max, j + 1)
                    nc.scalar.activation(tile, tile, ACT.Exp, bias=negm[:, pair, col:col + 1],
                                         accum_out=den[:, pair, col:col + 1]).then_inc(b_exp1, 1)

                def log_sum(unit, pair, j):
                    act.wait_ge(b_exp1, FREE + j + 1)
                    nc.scalar.activation(lnden[:, pair, :], den[:, pair, :], ACT.Ln).then_inc(b_ln, 1)

                def probabilities(i, s):
                    n = STEPS * i + s
                    act.wait_ge(b_s2, n + 1)
                    act.wait_ge(b_pv, n + 1)
                    nc.scalar.activation(probs[:, s % RING, :, :], ps[:, bank_s2:bank_s2 + 2, :],
                                         ACT.Exp).then_inc(b_exp2, 1)

                def step(i, e, s):
                    probabilities(i, s)
                    ahead = tile_at(i, e, s + LEAD - 1)
                    if ahead is not None:
                        sum_exp(STEPS * i + s + LEAD - 1, *ahead)
                    if s == 9:
                        log_sum(2 * i + 1, 1, STEPS * i + 31)
                    if s == 25 and not last(i):
                        log_sum(2 * i + 2, 0, STEPS * i + 47)
                    if last(i) and s in (20, 24):
                        k = (s - 20) // 4
                        set_copy(act, k, k)

                for j in range(LEAD - 1):
                    sum_exp(j, 0, j // TPB, j % TPB, slots=3 if j < LEAD - 3 else 2)
                    if j == 16:
                        log_sum(0, 0, 15)
                body(act, step)

            @block.vector
            def _(dve):
                dve.sem_inc(b_ctx, 1)
                dve.sem_inc(c_y, FSET * FREE)

                def row_max(j, e, h, qt, slots=2):
                    pair_bank = s1_bank(j, qt, slots)
                    pair, col = h // 2, h % 2 * TPB + qt
                    dve.wait_ge(b_s1, j + 1)
                    nc.vector.tensor_reduce(negm[:, pair, col:col + 1], ps[:, pair_bank:pair_bank + 2, :],
                                            AX.XY, ALU.max, negate=True).then_inc(b_max, 1)

                def split_shift(unit, pair):
                    done = nchain * unit
                    out_part = [shift_parts[:, :, :, k].rearrange("p t h -> p h t") for k in range(NSH)]
                    by_head = [a[:, :].rearrange("p (h t) -> p h t", h=2) for a in (shift, shift_rest)]
                    dve.wait_ge(b_ln, unit + 1)
                    nc.vector.tensor_tensor(shift[:, :], negm[:, pair, :], lnden[:, pair, :],
                                            ALU.subtract).then_inc(b_chain, 1)
                    dve.wait_ge(b_chain, done + 1)
                    nc.vector.tensor_copy(out_part[0], by_head[0]).then_inc(b_chain, 1)
                    dve.wait_ge(b_chain, done + 2)
                    nc.vector.tensor_tensor(by_head[1], by_head[0], out_part[0], ALU.subtract).then_inc(b_chain, 1)
                    dve.wait_ge(b_chain, done + 3)
                    nc.vector.tensor_copy(out_part[1], by_head[1]).then_inc(b_chain, 1)
                    dve.wait_ge(b_chain, done + 4)
                    nc.vector.tensor_tensor(out_part[2], by_head[1], out_part[1], ALU.subtract).then_inc(b_parts, 1)

                def copy_rows(use, pair):
                    dve.wait_ge(b_misc, use + 1)
                    nc.vector.tensor_copy(shift_rows[pair][:, :],
                                          ps[0:2 * NSH, bank_misc, :].bitcast(BF16)).then_inc(b_read, 1)

                def keep_context(i, s):
                    pair, qh = s // 16, s // TPB % 2
                    dve.wait_ge(b_pv, RING + STEPS * i + s + 1)
                    nc.vector.tensor_copy(ctx_t[:, pair, qh * HT:(qh + 1) * HT],
                                          ps[:, bank_ctx, :]).then_inc(b_ctx, 1)

                def add_output(i, e, blk, half, k, use):
                    if k == 0:
                        return
                    dve.wait_ge(b_misc, use + 1)
                    rows = xs[:, bass.ds(i // KV * TPB + blk % 2 * HALF + 2 * half, 2), :]
                    nc.vector.tensor_tensor(rows, rows, ps[:, bank_misc, :].rearrange("p (k d) -> p k d", k=2),
                                            ALU.add).then_inc(b_read, 1)

                def add_bias(i):
                    rows = xs[:, bass.ts(i, 2), :]
                    dve.wait_ge(b_read, used(i, (1, 0)) + 1)
                    nc.vector.tensor_tensor(rows, rows, bo_row[:, :].unsqueeze(1).to_broadcast([P, 2, D]),
                                            ALU.add).then_inc(b_bias, 1)

                def step(i, e, s):
                    ahead = tile_at(i, e, s + LEAD)
                    if s == 13:
                        copy_rows(used(i, "shift"), 1)
                    if s == 29 and not last(i):
                        copy_rows(used(i, "next shift"), 0)
                    if ahead is not None:
                        row_max(STEPS * i + s + LEAD, *ahead)
                    if s == 21:
                        add_bias(i)
                    if s == 10:
                        split_shift(2 * i + 1, 1)
                    if s == 26 and not last(i):
                        split_shift(2 * i + 2, 0)
                    if s == 24:
                        dve.wait_ge(b_bias, i + 1)
                    if s > 0:
                        projected(add_output, i, e, s - 1)
                    elif not (isinstance(i, int) and i == 0):
                        projected(add_output, i - 1, 1 - e, STEPS - 1)
                    if s % TPB == TPB - 1:
                        keep_context(i, s)
                    if last(i) and s in (10, 14, 18, 22):
                        k = (s - 10) // 4
                        for u in range(FSET):
                            set_statistics(dve, k, k % 2, u)
                        for u in range(FSET):
                            set_aggregate(dve, k, k % 2, u)
                        set_variance(dve, k, k % 2)
                        if k > 0:
                            for u in range(FSET):
                                set_norm(dve, k - 1, (k - 1) % 2, u)

                for j in range(LEAD):
                    row_max(j, 0, j // TPB, j % TPB, slots=3 if j < LEAD - 3 else 2)
                    if j == 18:
                        split_shift(0, 0)
                    if j == 20:
                        copy_rows(0, 0)
                body(dve, step)
                projected(add_output, GROUPS - 1, 1, STEPS - 1)
                for s in range(TPB):
                    projected(add_output, GROUPS, 0, s)

        with nc.Block() as block:
            def pipelined_sets(eng, step):
                step(0, 0)
                with rounds(nc, eng, SETS - 5, 2, start=1) as k1:
                    for q in (1, 0):
                        step(k1 + (1 - q), q)
                for k in range(SETS - 5, SETS + 1):
                    step(k, k % 2)

            @block.sync
            def _(sp):
                for q in range(2):
                    sp.sem_inc(c_stored[q], 1)
                with rounds(nc, sp, SETS, 2) as k2:
                    for q in range(2):
                        k = k2 + q
                        sp.wait_ge(c_y, FSET * (FREE + k + 1))
                        sp.sem_inc(apart, 1)
                        sp.dma_start(out_t[:, bass.ts(k, FSET), :], y[:, q]).then_inc(c_stored[q], 16)
                for q in range(2):
                    sp.wait_ge(c_stored[q], 1 + 16 * SETS // 2)

            @block.gpsimd
            def _(pool):
                def step(k, q):
                    if real(k + 4):
                        set_rstd(pool, k + 4, q)

                pipelined_sets(pool, step)

            @block.vector
            def _(dve):


                def add_paths(k, q, u):
                    dve.wait_ge(c_out, FSET * (FREE + k) + u + 1)
                    nc.vector.tensor_tensor(y[:, q, u, :], xs[:, FSET * k + u, :],
                                            ps[:, bank_ff + FSET * q + u, 0:D], ALU.add).then_inc(c_y, 1)

                def step(k, q):
                    ff = ps[:, bank_ff + FSET * q:bank_ff + FSET * (q + 1), :]
                    h_shared, h_routed = ff[:, :, D:D + R], ff[:, :, D + R:D + NLR]
                    wide, pairs = [P, FSET, E], [P, FSET, E, E]
                    done = ngate * k
                    if real(k):
                        dve.wait_ge(c_ff, FREE + k + 1)
                        nc.vector.tensor_tensor(lg[:, q], ff[:, :, D + NLR:NF],
                                                br_row[:, :].unsqueeze(1).to_broadcast(wide),
                                                ALU.add).then_inc(c_gate, 1)
                    if real(k + 4):
                        set_statistics(dve, k + 4, q, 0)
                    if real(k):
                        dve.wait_ge(c_gate, done + 1)
                    if real(k - 1):
                        dve.wait_ge(c_stored[1 - q], 1 + 16 * ((k - 1) // 2))
                    if real(k):
                        nc.vector.tensor_reduce(lmax[:, q], lg[:, q], AX.X, ALU.max).then_inc(c_gate, 1)
                    if real(k + 4):
                        set_statistics(dve, k + 4, q, 1)
                    if real(k):
                        dve.wait_ge(c_gate, done + 2)
                        nc.vector.tensor_tensor(lexp[:, q], lg[:, q], lmax[:, q].unsqueeze(2).to_broadcast(wide),
                                                ALU.subtract).then_inc(c_shifted, 1)
                    if real(k + 4):
                        set_aggregate(dve, k + 4, q, 0)
                        set_aggregate(dve, k + 4, q, 1)
                    if real(k):
                        dve.wait_ge(c_exp, k + 1)
                        nc.vector.tensor_reduce(lsum[:, q], lexp[:, q], AX.X, ALU.add).then_inc(c_gate, 1)
                    if real(k + 4):
                        set_variance(dve, k + 4, q)
                    if real(k):
                        dve.wait_ge(c_gate, done + 3)
                        nc.vector.reciprocal(linv[:, q], lsum[:, q]).then_inc(c_gate, 1)
                    if real(k - 1):
                        add_paths(k - 1, 1 - q, 0)
                    if real(k):
                        dve.wait_ge(c_gate, done + 4)
                        nc.vector.tensor_tensor(gates[:, q], lexp[:, q],
                                                linv[:, q].unsqueeze(2).to_broadcast(wide),
                                                ALU.mult).then_inc(c_gate, 1)
                    if real(k - 1):
                        add_paths(k - 1, 1 - q, 1)
                    if real(k):
                        dve.wait_ge(c_gate, done + 5)
                        other = gates[:, q].unsqueeze(2).to_broadcast(pairs)
                        own = gates[:, q].unsqueeze(3).to_broadcast(pairs)
                        nc.vector.tensor_tensor(above[:, q, :, :, 0, :], other, own, ALU.is_ge).then_inc(c_gate, 1)
                        nc.vector.tensor_tensor(above[:, q, :, :, 1, :], other, own, ALU.is_gt).then_inc(c_gate, 1)
                        dve.wait_ge(c_ht, FREE + k - 1)
                        nc.vector.tensor_copy(hw[:, q, :, 0:R], h_shared).then_inc(c_hw, 1)
                        dve.wait_ge(c_gate, done + 7)
                        both = above[:, q].rearrange("p f e c j -> p f (e c j)")
                        nc.vector.tensor_tensor(both, both, masks_sb[:, :].unsqueeze(1).to_broadcast(
                            [P, FSET, E * 2 * E]), ALU.mult).then_inc(c_gate, 1)
                    if real(k + 3):
                        set_norm(dve, k + 3, 1 - q, 0)
                    if real(k):
                        dve.wait_ge(c_gate, done + 8)
                        nc.vector.tensor_reduce(rank[:, q], above[:, q].rearrange("p f e c j -> p f e (c j)"),
                                                AX.X, ALU.add).then_inc(c_gate, 1)
                    if real(k + 3):
                        set_norm(dve, k + 3, 1 - q, 1)
                    if real(k):
                        dve.wait_ge(c_gate, done + 9)
                        nc.vector.scalar_tensor_tensor(out=wexp[:, q], in0=rank[:, q], scalar=float(TOP_K),
                                                       in1=gates[:, q], op0=ALU.is_lt,
                                                       op1=ALU.mult).then_inc(c_wexp, 1)
                        dve.wait_ge(c_wexp, k + 1)
                        nc.vector.tensor_tensor(hw[:, q, :, R:NLR].rearrange("p f (e r) -> p f e r", r=R),
                                                h_routed.rearrange("p f (e r) -> p f e r", r=R),
                                                wexp[:, q].unsqueeze(3).to_broadcast([P, FSET, E, R]),
                                                ALU.mult).then_inc(c_hw, 1)

                pipelined_sets(dve, step)

            @block.scalar
            def _(act):


                def step(k, q):
                    if real(k - 1):
                        act.wait_ge(c_ht, FREE + k)
                        act.wait_ge(c_out, FSET * (FREE + k - 2))
                        nc.scalar.copy(hw_t[:, 1 - q].rearrange("p f n -> p (f n)"),
                                       ps[0:NLR + 1, bank_ht + 1 - q, 0:FSET * P]).then_inc(c_hts, 1)
                    if real(k):
                        act.wait_ge(c_shifted, k + 1)
                        nc.scalar.activation(lexp[:, q], lexp[:, q], ACT.Exp).then_inc(c_exp, 1)
                    if real(k + 2):
                        set_copy(act, k + 2, q)

                pipelined_sets(act, step)

            @block.tensor
            def _(pe):
                def first_products(k, q):
                    pe.wait_ge(c_xts, FREE + k + 1)
                    for u in range(FSET):
                        pe.wait_ge(c_y, FSET * (FREE + k - 2) + u + 1)
                        for c in range(DC):
                            mm = nc.tensor.matmul(ps[:, bank_ff + FSET * q + u, 0:NF],
                                                  xhat_t[:, FSET * q + u, c, :],
                                                  wf[:, c, :], start=(c == 0), stop=(c == DC - 1))
                    mm.then_inc(c_ff, 1)

                def step(k, q):
                    if real(k - 1):
                        pe.wait_ge(c_hw, 2 * k)
                        pe.wait_ge(c_hts, FREE + k - 2)
                        for f in range(FSET):
                            mm = nc.tensor.transpose(ps[0:NLR + 1, bank_ht + 1 - q, f * P:(f + 1) * P],
                                                     hw[:, 1 - q, f, :], id32[:, :])
                        mm.then_inc(c_ht, 1)
                    if real(k + 2):
                        set_transpose(pe, k + 2, q)
                    if real(k - 1):
                        pe.wait_ge(c_hts, FREE + k)
                        for f in range(FSET):
                            mm = nc.tensor.matmul(ps[:, bank_ff + FSET * (1 - q) + f, 0:D], hw_t[:, 1 - q, f, :],
                                                  wlr[:, :], start=False, stop=True, skip_group_check=True)
                            mm.then_inc(c_out, 1)
                    if real(k + 1):
                        first_products(k + 1, 1 - q)

                first_products(0, 0)
                pipelined_sets(pe, step)


_INS = ['L0_attn_x', 'L0_attn_W_attn', 'L0_attn_W_out', 'L0_attn_b_out', 'L0_ffn_W_base', 'L0_ffn_b_base',
        'L0_ffn_A_s', 'L0_ffn_B_s', 'L0_ffn_A_r', 'L0_ffn_B_r', 'L0_ffn_W_router', 'L0_ffn_b_router']


def kernel(**inputs):
    import numpy as _np
    import concourse.bacc as _bacc
    from concourse import mybir as _mybir
    from concourse.bass_utils import run_bass_kernel_spmd as _run

    f32 = _np.float32
    inv_freq = (f32(1.0) / _np.power(f32(10000.0), _np.arange(0, DK, 2, dtype=f32) / f32(DK))).astype(f32)
    ang = _np.arange(L, dtype=f32)[:, None] * inv_freq[None, :]
    cos, sin = _np.cos(ang), _np.sin(ang)
    table = _np.stack([_np.concatenate([cos, cos], 1), _np.concatenate([-sin, sin], 1)], 1)
    table = _np.ascontiguousarray(table.reshape(TPB, P, 2, DK).transpose(1, 0, 2, 3)).astype(f32)
    before = _np.tril(_np.ones((E, E), f32), -1)
    masks = _np.stack([before, before.T], 1).reshape(1, E * 2 * E)
    masks = _np.ascontiguousarray(_np.broadcast_to(masks, (P, E * 2 * E)))
    consts = {"rope": table, "ident": _np.eye(P, dtype=f32), "masks": masks}

    nc = _bacc.Bacc("TRN2", target_bir_lowering=False, num_devices=1)
    arrays, args = {}, []
    for name, a in [(n, _np.ascontiguousarray(inputs[n])) for n in _INS] + list(consts.items()):
        arrays[f"in_{name}_dram"] = a
        args.append(nc.dram_tensor(f"in_{name}_dram", a.shape, _mybir.dt.from_np(a.dtype), kind="ExternalInput").ap())
    args.append(nc.dram_tensor("out_0_dram", (B, L, D), F32, kind="ExternalOutput").ap())
    layer_kernel(nc, *args)
    r = _run(nc, [arrays], core_ids=[0])
    return r.results[0]["out_0_dram"]
```
